# Optimizing a Trainium2 kernel written in Bass

```python
import numpy as np
import jax
import jax.numpy as jnp

def _softmax(x, axis=-1):
    return jax.nn.softmax(x, axis=axis)

def _gelu(x):
    return jax.nn.gelu(x, approximate=True)

def _silu(x):
    return jax.nn.silu(x)

def _sigmoid(x):
    return jax.nn.sigmoid(x)

def _layernorm(x, axis=-1, eps=1e-05):
    m = jnp.mean(x, axis=axis, keepdims=True)
    v = jnp.var(x, axis=axis, keepdims=True)
    return (x - m) / jnp.sqrt(v + eps)

def _scatter_add(tgt, idx, src, axis=0):
    return tgt.at[idx].add(src)

def _segment_sum(src, seg, n):
    return jax.ops.segment_sum(src, seg, n)
kernel_name = 'mk_flamingo_gated_d2_seqx_r8_d30ded'

def setup_inputs(seed: int=0):
    np.random.seed(seed)
    _w = jnp.asarray

    def _rec_inputs():
        import jax
        import jax.numpy as jnp
        _rk = jax.random.key(seed)
        x = 7.22e-05 + 1 * jax.random.normal(jax.random.fold_in(_rk, 1), (4, 512, 128), jnp.float32)
        _lenS = 512 - jax.random.randint(jax.random.fold_in(_rk, 7), (4,), 0, max(1, 512 // 4) + 1, jnp.int32)
        _lenS2 = 77 - jax.random.randint(jax.random.fold_in(_rk, 8), (4,), 0, max(1, 77 // 4) + 1, jnp.int32)
        _ctx_768P = jax.random.normal(jax.random.fold_in(_rk, 11), (4, 16, 96), jnp.float32)
        _ctx_768c = jax.random.dirichlet(jax.random.fold_in(_rk, 511), 0.3 * jnp.ones((16,), jnp.float32), (4, 77))
        _ctx_768t = jnp.einsum('bsk,bkd->bsd', _ctx_768c, _ctx_768P)
        _ctx_768t = _ctx_768t * jax.lax.rsqrt(jnp.mean(jnp.square(_ctx_768t)) + 1e-12) * 0.953939
        ctx_768 = 3.88148e-05 + 0.999967 * (_ctx_768t + 0.3 * jax.random.normal(jax.random.fold_in(_rk, 611), (4, 77, 96), jnp.float32))
        _validS = jnp.arange(512)[None, :] < _lenS[:, None]
        _validS2 = jnp.arange(77)[None, :] < _lenS2[:, None]
        _causal = jnp.tril(jnp.ones((512, 512), dtype=bool))
        mask_BxS_bf1 = jnp.ones((4, 512), dtype=bool)
        mask_BxS2_bf1 = jnp.ones((4, 77), dtype=bool)
        _g = jax.random.normal(jax.random.fold_in(_rk, 9001), (2, 2), jnp.float32)
        _g = jnp.sign(_g) * jnp.maximum(jnp.abs(_g), 1.0) + (_g == 0) * 1.0
        g_xattn = _g[0]
        g_ffn = _g[1]
        return (x, ctx_768, mask_BxS_bf1, mask_BxS2_bf1, g_xattn, g_ffn)
    x, ctx_768, mask_BxS_bf1, mask_BxS2_bf1, g_xattn, g_ffn = _rec_inputs()

    def _L0_xattn_setup():
        import jax, jax.numpy as jnp
        import numpy as np
        B, T, DT, G, DV = (16, 64, 128, 72, 96)
        H, DH = (4, 32)
        INNER = H * DH
        HID = 4 * DT
        N_STATE = 64
        K_TOP = 32

        def layernorm(x, g, b, eps=1e-05):
            m = x.mean(-1, keepdims=True)
            v = x.var(-1, keepdims=True)
            return (x - m) * jax.lax.rsqrt(v + eps) * g + b

        def s4d(x, log_dt, A_re, A_im, C_re, C_im, D_skip):
            Bb, L, D = x.shape
            dt = jnp.exp(log_dt)
            A = A_re + 1j * A_im
            C = C_re + 1j * C_im
            dtA = dt[:, None] * A
            dC = C * (jnp.exp(dtA) - 1.0) / A
            powers = jnp.exp(dtA[:, :, None] * jnp.arange(L))
            K = 2.0 * jnp.einsum('dn,dnl->dl', dC, powers).real
            n = 2 * L
            Kf = jnp.fft.rfft(K, n=n, axis=-1)
            xf = jnp.fft.rfft(x, n=n, axis=1)
            y = jnp.fft.irfft(xf * Kf.T[None], n=n, axis=1)[:, :L]
            return y + x * D_skip
        key = jax.random.key(seed)
        ks = jax.random.split(key, 16)
        s = 0.02
        inp = {'x_text': jax.random.normal(ks[0], (B, T, DT), jnp.float32), 'x_vision': jax.random.normal(ks[1], (B, G, DV), jnp.float32), 'text_mask': jnp.ones((B, T), bool), 'vision_mask': jnp.ones((B, G), bool), 'Wq': jax.random.normal(ks[2], (DT, INNER), jnp.float32) * s, 'Wk': jax.random.normal(ks[3], (DV, INNER), jnp.float32) * s, 'Wv': jax.random.normal(ks[4], (DV, DT), jnp.float32) * s, 'W_film_in': jax.random.normal(ks[5], (DT, 2 * DT), jnp.float32) * s, 'b_film_in': jnp.zeros((2 * DT,), jnp.float32), 'W_film_out': jax.random.normal(ks[6], (DT, 2 * DT), jnp.float32) * s, 'b_film_out': jnp.zeros((2 * DT,), jnp.float32), 'g_norm_in': jnp.ones((DT,), jnp.float32), 'b_norm_in': jnp.zeros((DT,), jnp.float32), 'g_norm_out': jnp.ones((DT,), jnp.float32), 'b_norm_out': jnp.zeros((DT,), jnp.float32), 'g_ffn': jnp.ones((DT,), jnp.float32), 'b_ffn': jnp.zeros((DT,), jnp.float32), 'W1': jax.random.normal(ks[7], (DT, HID), jnp.float32) * s, 'b1': jnp.zeros((HID,), jnp.float32), 'W2': jax.random.normal(ks[8], (HID, DT), jnp.float32) * s, 'b2': jnp.zeros((DT,), jnp.float32), 'log_dt': jnp.log(0.001) + jax.random.uniform(ks[9], (DT,), jnp.float32) * (jnp.log(0.1) - jnp.log(0.001)), 'A_re': -0.5 * jnp.ones((DT, N_STATE), jnp.float32), 'A_im': jnp.tile(jnp.pi * jnp.arange(N_STATE, dtype=jnp.float32), (DT, 1)), 'C_re': jax.random.normal(ks[10], (DT, N_STATE), jnp.float32) * 0.5 ** 0.5, 'C_im': jax.random.normal(ks[11], (DT, N_STATE), jnp.float32) * 0.5 ** 0.5, 'D_skip': jax.random.normal(ks[12], (DT,), jnp.float32), 'mod_gate': jnp.array(0.5, jnp.float32)}
        return inp
    _L0_xattn_all = _L0_xattn_setup()
    _L0_xattn_in = {k: v for k, v in _L0_xattn_all.items() if k in ('Wq', 'Wk', 'Wv', 'W_film_in', 'b_film_in', 'W_film_out', 'b_film_out', 'g_norm_in', 'b_norm_in', 'g_norm_out', 'b_norm_out', 'g_ffn', 'b_ffn', 'W1', 'b1', 'W2', 'b2', 'log_dt', 'A_re', 'A_im', 'C_re', 'C_im', 'D_skip', 'mod_gate')}
    del _L0_xattn_all

    def _L0_ffn_setup():
        import jax, jax.numpy as jnp
        import numpy as np
        D_MODEL = 128
        EXPANSION = 4
        D_HIDDEN = D_MODEL * EXPANSION
        NUM_STAGES = int(np.log2(D_HIDDEN))

        def butterfly(y, weights, dim):
            lead = y.shape[:-1]
            for stage in range(weights.shape[0]):
                s = 2 ** stage
                nb = dim // (2 * s)
                yr = y.reshape(*lead, nb, 2, s)
                a = yr[..., 0, :]
                b = yr[..., 1, :]
                w = weights[stage].reshape(nb, s, 2, 2)
                na = w[..., 0, 0] * a + w[..., 0, 1] * b
                nb2 = w[..., 1, 0] * a + w[..., 1, 1] * b
                y = jnp.stack([na, nb2], axis=-2).reshape(*lead, dim)
            return y
        key = jax.random.key(seed)
        ks = jax.random.split(key, 6)
        B, S = (4, 256)
        x = jax.random.normal(ks[0], (B, S, D_MODEL), jnp.float32)
        W_exp = jax.random.normal(ks[1], (D_MODEL, D_HIDDEN), jnp.float32) * 0.02
        b_exp = jnp.zeros((D_HIDDEN,), jnp.float32)
        up_weights = jax.random.normal(ks[2], (NUM_STAGES, D_HIDDEN // 2, 2, 2), jnp.float32) * 0.02
        up_bias = jnp.zeros((D_HIDDEN,), jnp.float32)
        down_weights = jax.random.normal(ks[3], (NUM_STAGES, D_HIDDEN // 2, 2, 2), jnp.float32) * 0.02
        W_con = jax.random.normal(ks[4], (D_HIDDEN, D_MODEL), jnp.float32) * 0.02
        b_con = jnp.zeros((D_MODEL,), jnp.float32)
        down_bias = jnp.zeros((D_MODEL,), jnp.float32)
        return dict(x=x, W_exp=W_exp, b_exp=b_exp, up_weights=up_weights, up_bias=up_bias, down_weights=down_weights, W_con=W_con, b_con=b_con, down_bias=down_bias)
    _L0_ffn_all = _L0_ffn_setup()
    _L0_ffn_in = {k: v for k, v in _L0_ffn_all.items() if k in ('W_exp', 'b_exp', 'up_weights', 'up_bias', 'down_weights', 'W_con', 'b_con', 'down_bias')}
    del _L0_ffn_all

    def _L1_xattn_setup():
        import jax, jax.numpy as jnp
        import numpy as np
        IN_DIM = 128
        CTX_DIM = 96
        NUM_HEADS = 16
        HEAD_DIM = IN_DIM // NUM_HEADS
        SCALE = 1.0 / float(np.sqrt(HEAD_DIM))
        key = jax.random.key(seed)
        ks = jax.random.split(key, 10)
        B, NQ, NKV = (8, 128, 64)
        s_in = 1.0 / float(np.sqrt(IN_DIM))
        s_ctx = 1.0 / float(np.sqrt(CTX_DIM))
        return {'x': jax.random.normal(ks[0], (B, NQ, IN_DIM), dtype=jnp.float32), 'context': jax.random.normal(ks[1], (B, NKV, CTX_DIM), dtype=jnp.float32), 'Wq': jax.random.normal(ks[2], (IN_DIM, IN_DIM), dtype=jnp.float32) * s_in, 'bq': jax.random.normal(ks[3], (IN_DIM,), dtype=jnp.float32) * 0.01, 'Wk': jax.random.normal(ks[4], (IN_DIM, CTX_DIM), dtype=jnp.float32) * s_ctx, 'bk': jax.random.normal(ks[5], (IN_DIM,), dtype=jnp.float32) * 0.01, 'Wv': jax.random.normal(ks[6], (IN_DIM, CTX_DIM), dtype=jnp.float32) * s_ctx, 'bv': jax.random.normal(ks[7], (IN_DIM,), dtype=jnp.float32) * 0.01, 'Wo': jax.random.normal(ks[8], (IN_DIM, IN_DIM), dtype=jnp.float32) * s_in, 'bo': jax.random.normal(ks[9], (IN_DIM,), dtype=jnp.float32) * 0.01}
    _L1_xattn_all = _L1_xattn_setup()
    _L1_xattn_in = {k: v for k, v in _L1_xattn_all.items() if k in ('Wq', 'bq', 'Wk', 'bk', 'Wv', 'bv', 'Wo', 'bo')}
    del _L1_xattn_all

    def _L1_ffn_setup():
        import jax, jax.numpy as jnp
        import numpy as np
        B, N, D, E, R, K = (4, 256, 128, 8, 32, 2)
        key = jax.random.key(seed)
        ks = jax.random.split(key, 5)
        scale = 0.02
        return {'x': jax.random.normal(ks[0], (B, N, D), dtype=jnp.float32), 'gate_w': jax.random.normal(ks[1], (D, E), dtype=jnp.float32) * scale, 'Wu': jax.random.normal(ks[2], (E, D, R), dtype=jnp.float32) * scale, 'Wv': jax.random.normal(ks[3], (E, D, R), dtype=jnp.float32) * scale, 'Wo': jax.random.normal(ks[4], (E, R, D), dtype=jnp.float32) * scale}
    _L1_ffn_all = _L1_ffn_setup()
    _L1_ffn_in = {k: v for k, v in _L1_ffn_all.items() if k in ('gate_w', 'Wu', 'Wv', 'Wo')}
    del _L1_ffn_all
    return {'x': x, 'ctx_768': ctx_768, 'mask_BxS_bf1': mask_BxS_bf1, 'mask_BxS2_bf1': mask_BxS2_bf1, 'g_xattn': g_xattn, 'g_ffn': g_ffn, 'L0_xattn_Wq': _L0_xattn_in['Wq'], 'L0_xattn_Wk': _L0_xattn_in['Wk'], 'L0_xattn_Wv': _L0_xattn_in['Wv'], 'L0_xattn_W_film_in': _L0_xattn_in['W_film_in'], 'L0_xattn_b_film_in': _L0_xattn_in['b_film_in'], 'L0_xattn_W_film_out': _L0_xattn_in['W_film_out'], 'L0_xattn_b_film_out': _L0_xattn_in['b_film_out'], 'L0_xattn_g_norm_in': _L0_xattn_in['g_norm_in'], 'L0_xattn_b_norm_in': _L0_xattn_in['b_norm_in'], 'L0_xattn_g_norm_out': _L0_xattn_in['g_norm_out'], 'L0_xattn_b_norm_out': _L0_xattn_in['b_norm_out'], 'L0_xattn_g_ffn': _L0_xattn_in['g_ffn'], 'L0_xattn_b_ffn': _L0_xattn_in['b_ffn'], 'L0_xattn_W1': _L0_xattn_in['W1'], 'L0_xattn_b1': _L0_xattn_in['b1'], 'L0_xattn_W2': _L0_xattn_in['W2'], 'L0_xattn_b2': _L0_xattn_in['b2'], 'L0_xattn_log_dt': _L0_xattn_in['log_dt'], 'L0_xattn_A_re': _L0_xattn_in['A_re'], 'L0_xattn_A_im': _L0_xattn_in['A_im'], 'L0_xattn_C_re': _L0_xattn_in['C_re'], 'L0_xattn_C_im': _L0_xattn_in['C_im'], 'L0_xattn_D_skip': _L0_xattn_in['D_skip'], 'L0_xattn_mod_gate': _L0_xattn_in['mod_gate'], 'L0_ffn_W_exp': _L0_ffn_in['W_exp'], 'L0_ffn_b_exp': _L0_ffn_in['b_exp'], 'L0_ffn_up_weights': _L0_ffn_in['up_weights'], 'L0_ffn_up_bias': _L0_ffn_in['up_bias'], 'L0_ffn_down_weights': _L0_ffn_in['down_weights'], 'L0_ffn_W_con': _L0_ffn_in['W_con'], 'L0_ffn_b_con': _L0_ffn_in['b_con'], 'L0_ffn_down_bias': _L0_ffn_in['down_bias'], 'L1_xattn_Wq': _L1_xattn_in['Wq'], 'L1_xattn_bq': _L1_xattn_in['bq'], 'L1_xattn_Wk': _L1_xattn_in['Wk'], 'L1_xattn_bk': _L1_xattn_in['bk'], 'L1_xattn_Wv': _L1_xattn_in['Wv'], 'L1_xattn_bv': _L1_xattn_in['bv'], 'L1_xattn_Wo': _L1_xattn_in['Wo'], 'L1_xattn_bo': _L1_xattn_in['bo'], 'L1_ffn_gate_w': _L1_ffn_in['gate_w'], 'L1_ffn_Wu': _L1_ffn_in['Wu'], 'L1_ffn_Wv': _L1_ffn_in['Wv'], 'L1_ffn_Wo': _L1_ffn_in['Wo']}

def reference(x, ctx_768, mask_BxS_bf1, mask_BxS2_bf1, g_xattn, g_ffn, L0_xattn_Wq, L0_xattn_Wk, L0_xattn_Wv, L0_xattn_W_film_in, L0_xattn_b_film_in, L0_xattn_W_film_out, L0_xattn_b_film_out, L0_xattn_g_norm_in, L0_xattn_b_norm_in, L0_xattn_g_norm_out, L0_xattn_b_norm_out, L0_xattn_g_ffn, L0_xattn_b_ffn, L0_xattn_W1, L0_xattn_b1, L0_xattn_W2, L0_xattn_b2, L0_xattn_log_dt, L0_xattn_A_re, L0_xattn_A_im, L0_xattn_C_re, L0_xattn_C_im, L0_xattn_D_skip, L0_xattn_mod_gate, L0_ffn_W_exp, L0_ffn_b_exp, L0_ffn_up_weights, L0_ffn_up_bias, L0_ffn_down_weights, L0_ffn_W_con, L0_ffn_b_con, L0_ffn_down_bias, L1_xattn_Wq, L1_xattn_bq, L1_xattn_Wk, L1_xattn_bk, L1_xattn_Wv, L1_xattn_bv, L1_xattn_Wo, L1_xattn_bo, L1_ffn_gate_w, L1_ffn_Wu, L1_ffn_Wv, L1_ffn_Wo):
    import jax
    import jax.numpy as jnp

    def _L0_xattn_ref(x_text, x_vision, text_mask, vision_mask, Wq, Wk, Wv, W_film_in, b_film_in, W_film_out, b_film_out, g_norm_in, b_norm_in, g_norm_out, b_norm_out, g_ffn, b_ffn, W1, b1, W2, b2, log_dt, A_re, A_im, C_re, C_im, D_skip, mod_gate):
        import jax, jax.numpy as jnp
        import numpy as np
        B, T, DT, G, DV = (16, 64, 128, 72, 96)
        H, DH = (4, 32)
        INNER = H * DH
        HID = 4 * DT
        N_STATE = 64
        K_TOP = 32

        def layernorm(x, g, b, eps=1e-05):
            m = x.mean(-1, keepdims=True)
            v = x.var(-1, keepdims=True)
            return (x - m) * jax.lax.rsqrt(v + eps) * g + b

        def s4d(x, log_dt, A_re, A_im, C_re, C_im, D_skip):
            Bb, L, D = x.shape
            dt = jnp.exp(log_dt)
            A = A_re + 1j * A_im
            C = C_re + 1j * C_im
            dtA = dt[:, None] * A
            dC = C * (jnp.exp(dtA) - 1.0) / A
            powers = jnp.exp(dtA[:, :, None] * jnp.arange(L))
            K = 2.0 * jnp.einsum('dn,dnl->dl', dC, powers).real
            n = 2 * L
            Kf = jnp.fft.rfft(K, n=n, axis=-1)
            xf = jnp.fft.rfft(x, n=n, axis=1)
            y = jnp.fft.irfft(xf * Kf.T[None], n=n, axis=1)[:, :L]
            return y + x * D_skip
        Bb, Tt, D = x_text.shape
        Gg = x_vision.shape[1]
        Q = (x_text @ Wq).reshape(Bb, Tt, H, DH)
        K = (x_vision @ Wk).reshape(Bb, Gg, H, DH)
        scores = jnp.einsum('bthd,bghd->bhtg', Q, K) / np.sqrt(DH).astype(np.float32)
        scores = jnp.where(vision_mask[:, None, None, :], scores, -jnp.inf)
        topv, topi = jax.lax.top_k(scores, K_TOP)
        probs = jax.nn.softmax(topv, axis=-1)
        bi = jnp.arange(Bb)[:, None, None, None]
        hi = jnp.arange(H)[None, :, None, None]
        ti = jnp.arange(Tt)[None, None, :, None]
        attn = jnp.zeros_like(scores).at[bi, hi, ti, topi].set(probs)
        attn_mean = attn.mean(axis=1)
        V = x_vision @ Wv
        c_t = jnp.einsum('btg,bgd->btd', attn_mean, V)
        c_t = c_t * text_mask[..., None]
        x = layernorm(x_text, g_norm_in, b_norm_in)
        scale_in, shift_in = jnp.split(c_t @ W_film_in + b_film_in, 2, axis=-1)
        x = x * (1.0 + mod_gate * scale_in) + mod_gate * shift_in
        y = s4d(x, log_dt, A_re, A_im, C_re, C_im, D_skip)
        scale_out, shift_out = jnp.split(c_t @ W_film_out + b_film_out, 2, axis=-1)
        y = y * (1.0 + mod_gate * scale_out) + mod_gate * shift_out
        xt = x_text + y
        h = layernorm(xt, g_ffn, b_ffn)
        h = jax.nn.gelu(h @ W1 + b1, approximate=False) @ W2 + b2
        xt = xt + h
        return layernorm(xt, g_norm_out, b_norm_out)

    def _L0_ffn_ref(x, W_exp, b_exp, up_weights, up_bias, down_weights, W_con, b_con, down_bias):
        import jax, jax.numpy as jnp
        import numpy as np
        D_MODEL = 128
        EXPANSION = 4
        D_HIDDEN = D_MODEL * EXPANSION
        NUM_STAGES = int(np.log2(D_HIDDEN))

        def butterfly(y, weights, dim):
            lead = y.shape[:-1]
            for stage in range(weights.shape[0]):
                s = 2 ** stage
                nb = dim // (2 * s)
                yr = y.reshape(*lead, nb, 2, s)
                a = yr[..., 0, :]
                b = yr[..., 1, :]
                w = weights[stage].reshape(nb, s, 2, 2)
                na = w[..., 0, 0] * a + w[..., 0, 1] * b
                nb2 = w[..., 1, 0] * a + w[..., 1, 1] * b
                y = jnp.stack([na, nb2], axis=-2).reshape(*lead, dim)
            return y
        h = jnp.einsum('bsd,dh->bsh', x, W_exp) + b_exp
        h = butterfly(h, up_weights, D_HIDDEN)
        h = jax.nn.gelu(h + up_bias, approximate=False)
        h = butterfly(h, down_weights, D_HIDDEN)
        y = jnp.einsum('bsh,hd->bsd', h, W_con) + b_con
        return y + down_bias

    def _L1_xattn_ref(x, context, Wq, bq, Wk, bk, Wv, bv, Wo, bo):
        import jax, jax.numpy as jnp
        import numpy as np
        IN_DIM = 128
        CTX_DIM = 96
        NUM_HEADS = 16
        HEAD_DIM = IN_DIM // NUM_HEADS
        SCALE = 1.0 / float(np.sqrt(HEAD_DIM))
        q = x @ Wq.T + bq
        k = context @ Wk.T + bk
        v = context @ Wv.T + bv
        B, NQ, _ = q.shape
        NKV = k.shape[1]
        q = q.reshape(B, NQ, NUM_HEADS, HEAD_DIM)
        k = k.reshape(B, NKV, NUM_HEADS, HEAD_DIM)
        v = v.reshape(B, NKV, NUM_HEADS, HEAD_DIM)
        attn = jnp.einsum('bihd,bjhd->bhij', q, k) * SCALE
        attn = jax.nn.softmax(attn, axis=-1)
        out = jnp.einsum('bhij,bjhd->bihd', attn, v)
        out = out.reshape(B, NQ, IN_DIM)
        return out @ Wo.T + bo

    def _L1_ffn_ref(x, gate_w, Wu, Wv, Wo):
        import jax, jax.numpy as jnp
        import numpy as np
        B, N, D, E, R, K = (4, 256, 128, 8, 32, 2)
        logits = jnp.einsum('bnd,de->bne', x, gate_w)
        topv, topi = jax.lax.top_k(logits, K)
        w = jax.nn.softmax(topv, axis=-1)
        u = jnp.einsum('bnd,edr->bner', x, Wu)
        v = jnp.einsum('bnd,edr->bner', x, Wv)
        s = jax.nn.silu(u) * v
        Y = jnp.einsum('bner,erd->bned', s, Wo)
        y_sel = jnp.take_along_axis(Y, topi[..., None], axis=2)
        out = jnp.einsum('bnkd,bnk->bnd', y_sel, w)
        return out
    x = x + jnp.tanh(g_xattn[0]) * _L0_xattn_ref(_layernorm(x, axis=-1), ctx_768, mask_BxS_bf1, mask_BxS2_bf1, L0_xattn_Wq, L0_xattn_Wk, L0_xattn_Wv, L0_xattn_W_film_in, L0_xattn_b_film_in, L0_xattn_W_film_out, L0_xattn_b_film_out, L0_xattn_g_norm_in, L0_xattn_b_norm_in, L0_xattn_g_norm_out, L0_xattn_b_norm_out, L0_xattn_g_ffn, L0_xattn_b_ffn, L0_xattn_W1, L0_xattn_b1, L0_xattn_W2, L0_xattn_b2, L0_xattn_log_dt, L0_xattn_A_re, L0_xattn_A_im, L0_xattn_C_re, L0_xattn_C_im, L0_xattn_D_skip, L0_xattn_mod_gate)
    x = x + jnp.tanh(g_ffn[0]) * _L0_ffn_ref(_layernorm(x, axis=-1), L0_ffn_W_exp, L0_ffn_b_exp, L0_ffn_up_weights, L0_ffn_up_bias, L0_ffn_down_weights, L0_ffn_W_con, L0_ffn_b_con, L0_ffn_down_bias)
    x = x + jnp.tanh(g_xattn[1]) * _L1_xattn_ref(_layernorm(x, axis=-1), ctx_768, L1_xattn_Wq, L1_xattn_bq, L1_xattn_Wk, L1_xattn_bk, L1_xattn_Wv, L1_xattn_bv, L1_xattn_Wo, L1_xattn_bo)
    x = x + jnp.tanh(g_ffn[1]) * _L1_ffn_ref(_layernorm(x, axis=-1), L1_ffn_gate_w, L1_ffn_Wu, L1_ffn_Wv, L1_ffn_Wo)
    return x

_drawn_inputs = setup_inputs


def setup_inputs(seed=0):
    import zlib

    import numpy as np

    out = dict(_drawn_inputs(seed))
    spreads = {'g_ffn': (-1.0, 0.6),
     'L0_xattn_b_film_in': (0.0, 0.273),
     'L0_xattn_b_film_out': (0.0, 0.303),
     'L0_xattn_g_norm_in': (1.0, 0.2),
     'L0_xattn_b_norm_in': (0.0, 0.1),
     'L0_xattn_g_norm_out': (1.0, 0.2),
     'L0_xattn_b_norm_out': (0.0, 0.1),
     'L0_xattn_g_ffn': (1.0, 0.6),
     'L0_xattn_b_ffn': (0.0, 0.8),
     'L0_xattn_b1': (0.0, 0.8),
     'L0_xattn_b2': (0.0, 0.342),
     'L0_xattn_A_re': (-0.5, 0.2),
     'L0_ffn_b_exp': (0.0, 0.1),
     'L0_ffn_up_bias': (0.0, 0.1),
     'L0_ffn_b_con': (0.0, 0.1),
     'L0_ffn_down_bias': (0.0, 0.1)}
    factors = {'L0_xattn_Wq': 8.0,
     'L0_xattn_Wk': 8.0,
     'L0_xattn_Wv': 6.098,
     'L0_xattn_W_film_in': 7.024,
     'L0_xattn_W_film_out': 8.0,
     'L0_xattn_W1': 4.164,
     'L0_xattn_W2': 3.82,
     'L1_xattn_bq': 8.0,
     'L1_xattn_bk': 8.0,
     'L1_xattn_bv': 8.0,
     'L1_xattn_bo': 8.0,
     'L1_ffn_gate_w': 8.0,
     'L1_ffn_Wu': 8.0,
     'L1_ffn_Wv': 8.0,
     'L1_ffn_Wo': 8.0}
    for name, (base, spread) in spreads.items():
        noise = np.random.default_rng([zlib.crc32(name.encode()), seed]).standard_normal(out[name].shape)
        drawn = base * np.exp(spread * noise) if base else spread * noise
        out[name] = jnp.asarray(drawn.astype(out[name].dtype))
    for name, factor in factors.items():
        out[name] = (out[name] * factor).astype(out[name].dtype)
    return out
```

```python
from contextlib import ExitStack

import numpy as np

import concourse.bass as bass
from concourse import mybir

B, S, D = 4, 512, 128
P = 128
NT = S // P
SK, DC = 77, 96
H0, DH0, TOPK = 4, 32, 32
H1, DH1 = 16, 8
HID = 512
HT = HID // P
NE, RE = 8, 32
NS = 64
L1, L2 = 32, 16
CH = 256
EPS = 1e-5
NEG = -3.0e38
MASKED = -1.0e30
MAGIC = 12582912.0
GROUPS = [(0, 6), (6, 6), (12, 4)]
FLAT = H1 * SK
NCH = (FLAT + P - 1) // P
CROWS = [min(P, FLAT - P * c) for c in range(NCH)]
CH0 = [(P * c) // SK for c in range(NCH)]
CHN = [min(3, H1 - h) for h in CH0]
VW9 = DH1 + 1
LOW, HIGH = 5, 4
NB = 9



def columns(parts):
    at, out = 0, {}
    for name, n in parts:
        out[name] = (at, at + n)
        at += n
    return out, at


SMALL, N_SMALL = columns([
    ("mod_gate", 1), ("gx0", 1), ("gf0", 1), ("gx1", 1), ("gf1", 1),
    ("gin", 1), ("bin", 1), ("bfilm", 4), ("film_one", 4), ("gffn", 1), ("bffn", 1), ("b1", 4), ("b2", 1),
    ("gno", 1), ("bno", 1), ("upb", 4), ("bcon", 1), ("dbias", 1), ("bq", 1), ("bo", 1),
    ("sin_off", 1), ("sgn2", 1), ("sgnf", 1), ("sin_bias", 1), ("hmask0", H0), ("hmask1", H1),
])
FIRST, N_FIRST = columns([("C", P), ("J", P), ("I", P), ("wqT0", P), ("wk0", P), ("ctx", B * SK)])
KGEN, N_KGEN = columns([("logdt", D), ("are", D), ("aim", D), ("c1", D), ("c2", D), ("l1row", L1), ("l2row", L2)])
FILM, N_FILM = columns([("wvT", DC), ("film", 4 * D)])
DFT, N_DFT = columns([("near", 4 * CH), ("icos", 2 * CH), ("isin", 2 * CH), ("tail", 4 * CH)])
FFN, N_FFN = columns([("w1", HID), ("w2", HID)])
BFLY, N_BFLY = columns([
    ("idl", 4 * 32), ("idh", 4 * 16), ("eye32", 32), ("eye4", 4),
    ("ulow", LOW * 256), ("dlow", LOW * 256), ("uhigh", HIGH * 128), ("dhigh", HIGH * 128),
    ("wexpT", HT * (P + 1)), ("wcon", HID),
])
ATT1, N_ATT1 = columns([("wkT", P), ("wqT", P), ("woT", P), ("wv9", H1 * VW9), ("vmask", NCH * 3 * VW9)])
MOE, N_MOE = columns([("gate", NE), ("wu", NE * RE), ("wv", NE * RE), ("wo", 2 * D), ("expand", NE * RE)])


ORDER = """
center0/0 s_cols s_k0 var0/0 s_m0 s_kgen0 s_kgen1 score0/0 score1/0 center0/1 s_kgen2 weigh0/0 score2/0 weigh1/0
score3/0 s_vw weigh2/0 s_w1 s_kern0 s_kern1 s_kern2 weigh3/0 center0/2 s_kern3 var0/1 attnT/0 vw/0 film_in/0
xt/0 dft/0 score0/1 s_freq s_bfly0 score1/1 mix/0 weigh0/1 score2/1 weigh1/1 idft/0 s_bfly1 film_out/0 var0/2
center1/0 var1/0 score3/1 weigh2/1 ffn_up/0 weigh3/1 score0/2 score1/2 attnT/1 ffn_down/0 vw/1 film_in/1 xt/1
dft/1 center2/0 weigh0/2 score2/2 mix/1 s_bfly2 weigh1/2 score3/2 var2/0 idft/1 film_out/1 s_bfly3 center0/3
center1/1 x1/0 var1/1 var0/3 center3/0 var3/0 weigh2/2 fold_up/0 weigh3/2 attnT/2 vw/2 fold_down/0 center4/0
score0/3 ffn_up/1 var4/0 ffn_down/1 film_in/2 center2/1 k1/0 xt/2 var2/1 score1/3 x1/1 dft/2 mix/2 weigh0/3 q/0
scoreA0/0 scoreA1/0 idft/2 s_v1 score2/3 mixA0/0 scoreA2/0 center3/1 weigh1/3 film_out/2 var3/1 mixA1/0 score3/3
weigh2/3 center1/2 fold_up/1 var1/2 fold_down/1 weigh3/3 s_misc ffn_up/2 attnT/3 vw/3 scoreA3/0 film_in/3
ffn_down/2 center4/1 mixA2/0 var4/1 center2/2 var2/2 x1/2 mixA3/0 center3/2 k1/1 xt/3 outT/0 var3/2 q/1 wo/0
dft/3 scoreA0/1 fold_up/2 mix/3 scoreA1/1 center5/0 idft/3 mixA0/1 var5/0 scoreA2/1 logits/0 film_out/3
fold_down/2 mixA1/1 scoreA3/1 center1/3 mixA2/1 mixA3/1 var1/3 outT/1 ffn_up/3 top2/0 ffn_down/3 center2/3
expand/0 experts/0 wo/1 var2/3 x1/3 center4/2 var4/2 center5/1 center3/3 var5/1 var3/3 logits/1 top2/1 fold_up/3
fold_down/3 moe_out/0 expand/1 k1/2 q/2 center4/3 experts/1 scoreA0/2 scoreA1/2 mixA0/2 scoreA2/2 var4/3 mixA1/2
scoreA3/2 k1/3 mixA2/2 q/3 mixA3/2 outT/2 wo/2 scoreA0/3 scoreA1/3 mixA0/3 scoreA2/3 mixA1/3 center5/2 scoreA3/3
moe_out/1 mixA2/3 mixA3/3 var5/2 outT/3 wo/3 logits/2 center5/3 top2/2 var5/3 logits/3 top2/3 expand/2 experts/2
expand/3 moe_out/2 experts/3 moe_out/3
"""
SCHEDULE = [(step, int(b or 0)) for step, _, b in (word.partition("/") for word in ORDER.split())]
CENTERS = [x for x in SCHEDULE if x[0].startswith("center")]
VARS = [x for x in SCHEDULE if x[0].startswith("var")]

PSUM_USE = {
    **{f"center{i}": [(f"cen{i}", f"var{i}")] for i in range(6)},
    **{f"var{i}": [(f"var{i}", f"var{i}")] for i in range(6)},
    **{f"score{t}": [(f"score{t}", f"score{t}")] for t in range(NT)},
    "attnT": [("attnT", "attnT")],
    "film_in": [("fa", "film_in"), ("fb", "film_in")],
    "xt": [("xt", "xt")],
    "dft": [("d0", "dft"), ("d1", "dft")],
    "idft": [("y", "film_out")],
    "film_out": [("fc", "film_out"), ("fd", "film_out")],
    "ffn_up": [(f"up{j}", "ffn_up") for j in range(HT)],
    "ffn_down": [("down", "ffn_down")],
    "fold_up": [(f"fup{j}", "fold_up") for j in range(HT)],
    "fold_down": [("fdown", "fold_down")],
    "q": [("q", "q")],
    **{f"scoreA{t}": [(f"sA{t}_{g}", f"scoreA{t}") for g in range(3)] for t in range(NT)},
    **{f"mixA{t}": [(f"tA{t}_{g}", f"mixA{t}") for g in range(3)] + [(f"oA{t}", f"mixA{t}")] for t in range(NT)},
    "outT": [("outT", "outT")],
    "wo": [("wo", "wo")],
    "logits": [("logits", "logits")],
    "expand": [("wT", "expand"), ("ex0", "experts"), ("ex1", "experts")],
    "experts": [("u0", "experts"), ("u1", "experts"), ("v0", "experts"), ("v1", "experts")],
    "moe_out": [("moe", "moe_out")],
    "s_k0": [("k0", "s_k0")], "s_m0": [(f"m0_{i}", "s_m0") for i in range(B)],
    "s_vw": [("wvf", "s_vw")], "vw": [("vw", "vw")],
    "s_w1": [("w1c", "s_w1")],
    **{f"s_kern{i}": [(f"kern{i}", f"s_kern{i}")] for i in range(4)},
    "s_freq": [("fr0", "s_freq"), ("fr1", "s_freq")],
    "s_bfly1": [(f"t1_{i}", "s_bfly1") for i in range(2)],
    "s_bfly2": [("wup", "s_bfly2"), ("bup", "s_bfly2"), ("t2", "s_bfly2")],
    "s_bfly3": [("wdn", "s_bfly3")],
    "k1": [("k1", "k1")], "s_v1": [("v1a", "s_v1"), ("v1b", "s_v1")],
}


def place_banks():
    free, held, bank, before, last = list(range(8)), [], {}, {}, {}
    for at, (step, b) in enumerate(SCHEDULE):
        for name, until in PSUM_USE.get(step, []):
            i = free.pop(0)
            bank[name, b] = i
            before[name, b] = last.get(i)
            last[i] = (name, b)
            held.append((until, b, i))
        for h in [h for h in held if h[:2] == (step, b)]:
            held.remove(h)
            free.append(h[2])
    return bank, before


BANK, BEFORE = place_banks()


def build(nc, dram, out_dram):
    f32, bf16 = mybir.dt.float32, mybir.dt.bfloat16
    u8 = mybir.dt.uint8
    ALU, ACT, AX = mybir.AluOpType, mybir.ActivationFunctionType, mybir.AxisListType

    ctx = ExitStack()
    with ctx:
        def sb(name, shape, dt=f32):
            return ctx.enter_context(nc.sbuf_tensor(name, shape, dt))

        def sem(name):
            return ctx.enter_context(nc.semaphore(name))

        packs = {}
        for name, cols, n in (("small", SMALL, N_SMALL), ("first", FIRST, N_FIRST), ("kgen", KGEN, N_KGEN),
                              ("film", FILM, N_FILM), ("dft", DFT, N_DFT), ("ffn", FFN, N_FFN),
                              ("bfly", BFLY, N_BFLY), ("att1", ATT1, N_ATT1), ("moe", MOE, N_MOE)):
            packs[name] = (sb(f"pack_{name}", [P, n]), cols)

        def part(pack, name, rows=P):
            t, cols = packs[pack]
            a, b = cols[name]
            return t[0:rows, a:b]

        X = sb("X", [P, B, S])
        vmask8 = sb("vmask8", [1, B * SK], u8)
        tmask8 = sb("tmask8", [P, B * NT], u8)
        tanhs = sb("tanhs", [P, 4])
        filmb = sb("filmb", [P, 4])
        gin2 = sb("gin2", [P, 1])
        gA, bA = sb("gA", [P, 1]), sb("bA", [P, 1])
        dskip = sb("dskip", [1, D])
        b1f, bup = sb("b1f", [P, HT]), sb("bup", [P, HT])
        bdn, bo1 = sb("bdn", [P, 1]), sb("bo1", [P, 1])
        tm4, cst = sb("tm4", [P, B * NT]), sb("cst", [P, 4])
        maskf, maskrow = sb("maskf", [1, B, SK]), sb("maskrow", [P, B, H0 * SK], bf16)
        ones_bf = sb("ones_bf", [P, P], bf16)
        M0 = sb("M0", [P, B, H0 * SK])
        wvf, VW = sb("wvf", [DC, 4 * D]), sb("VW", [SK, 2, 4 * D])
        v9 = sb("v9", [P, B, NCH, 3 * VW9])
        KT = sb("KT", [P, 4, D])
        bflyl, bflyh = sb("bflyl", [P, 2, 4, 32]), sb("bflyh", [P, 2, 4, 16])
        bt1, bt2 = sb("bt1", [P, 128]), sb("bt2", [P, 128])

        arena = sb("arena", [P, 4 * D * L1])

        def cut(t, at, *shape):
            n = int(np.prod(shape))
            axes = " ".join("abcd"[:len(shape)])
            flat = t[:, at:at + n]
            if len(shape) == 1:
                return flat
            return flat.rearrange(f"p ({axes}) -> p {axes}", **dict(zip("abcd"[1:len(shape)], shape[1:])))

        big = [cut(arena, D * L1 * i, D * L1) for i in range(4)]
        HIDB = cut(arena, 0, 2, HT, S)
        bdh, bdl = cut(arena, 4096, 4, HID), cut(arena, 6144, 4, P)
        t1s, t2s = cut(arena, 6656, 4, P + 1), cut(arena, 7172, 4, P)
        k1bd = cut(arena, 4096, 2, H1, SK)
        PR = cut(arena, 6560, 2, FLAT)
        PT = cut(arena, 9024, 2, NCH, P)
        SU = cut(arena, 11584, 2, S)
        XTM = cut(arena, 12608, 2, NT, D)
        XF = cut(arena, 13632, 2, 2, 2, D)
        YZ = cut(arena, 14656, 2, 2, 2, D)
        H0f = cut(packs["film"][0], 0, 2, 2, D)
        H1f = cut(packs["kgen"][0], 0, 2, 2, D)
        tail = DFT["tail"][0]
        wupf, wdnf = cut(packs["dft"][0], tail, HID), cut(packs["dft"][0], tail + HID, HT, D)
        w1g, woT1, wom = part("ffn", "w1"), part("att1", "woT"), part("moe", "wo").rearrange("p (j d) -> p j d", j=2)
        LG, LR = cut(arena, 15680, 2, NT, 14), cut(arena, 15792, 2, NT, 14)
        G8, GR, GE, GS, GW = (cut(arena, 15904 + 64 * i, 2, NT, 8) for i in range(5))
        k0bd_t = sb("k0bd", [P, FLAT])
        k0bd, ctxrep = cut(k0bd_t, 0, B, H0, SK), cut(k0bd_t, 0, B, 3 * SK)[0:DC + 1]
        pb = packs["bfly"][0]
        Q1, OT, OTT = cut(pb, 0, B, S), cut(pb, 2048, 2, NT, P), cut(pb, 3072, S)
        WT = pb[:, 3584:4096].bitcast(bf16).rearrange("p (b s) -> p b s", b=2)[0:3 * NE]
        expand = pb[:, 4096:4224].bitcast(bf16)[0:3 * NE]
        GB = pb[:, 4224:4288].bitcast(bf16).rearrange("p (b i t e) -> p b i t e", b=2, i=2, t=NT)
        G3 = cut(pb, 4288, 2, NT, 3 * NE)
        RS, LO = sb("RS", [P, 2, S]), sb("LO", [P, B, S])
        SQ = LO
        XN, XG, R12 = sb("XN", [P, 2, S]), sb("XG", [P, B, S]), sb("R12", [P, S])
        ASUM, AT = sb("ASUM", [P, 2, NT, SK]), sb("AT", [SK, 2, S])
        MT_t, AO = sb("MT", [P, 8 * 2 * D]), sb("AO", [P, S])
        MT = cut(MT_t, 0, 4, 2, 2 * D)
        names = ("dt", "a", "u", "k", "v", "th", "em", "q", "sb", "er", "ei", "m", "gr", "gi", "t1", "t2", "al", "be",
                 "t3", "t4")
        kt = {x: (MT_t[:, D * i:D * i + D] if i < 16 else AO[:, D * (i - 16):D * (i - 15)]) for i, x in enumerate(names)}
        V8, R8, E0 = sb("V8", [P, 2, H0, 4, 8]), sb("R8", [P, 2, 2, H0, SK]), sb("E0", [P, 2, H0, SK])
        negm, sel, sm = sb("negm", [P, 2, H0]), sb("sel", [P, 2, H0, SK]), sb("sm", [P, 3, H0])
        w4, dw, a2 = sb("w4", [P, 2, H0]), sb("dw", [P, H0, SK]), sb("a2", [P, 2, SK])
        mx1, rec1 = sb("mx1", [P, 2, H1]), sb("rec1", [P, 2, H1])
        gsum = sb("gsum", [P, 2, NT])

        psum = [ctx.enter_context(nc.psum_tensor(f"bank{i}", [P, 512], f32)) for i in range(8)]

        def bank(name, b):
            return psum[BANK[name, b]]

        x_loaded = [sem(f"x_loaded{b}") for b in range(B)]
        loaded = {n: sem(f"loaded_{n}") for n in packs}
        masks_loaded, stored = sem("masks_loaded"), sem("stored")
        centered, squared, variance, rs_done = sem("centered"), sem("squared"), sem("variance"), sem("rs_done")
        normed = [sem(f"normed{i}") for i in range(6)]
        x_ready = {n: sem(f"ready_{n}") for n in ("xt2", "xt3", "x1", "x2", "x3")}
        n = ["affined", "scores_ready", "topk_step", "negmax_ready", "exps_done", "selected", "weights_ready",
             "attn_summed", "attnT_ready", "attnT_copied", "film_in_ready", "filmed", "xt_ready", "xt_copied",
             "dft_ready", "dft_copied", "mixed_y", "mixed_z", "y_ready", "film_out_ready", "ao_ready",
             "up_ready", "up_gelu", "down_ready", "fup_ready", "fup_gelu", "fdown_ready", "scaled_out",
             "q_ready", "q_copied", "scoresA_ready", "shifted", "probs_ready", "probsT_ready", "probsT_copied",
             "pv_ready", "pv_scaled", "outT_ready", "outT_copied", "wo_ready", "logits_ready", "logits_copied",
             "shift_ready", "gate_exp", "gate_ready", "wT_ready", "wT_copied", "expand_ready", "u_ready",
             "v_ready", "silu_ready", "experts_ready", "moe_ready", "x4_ready",
             "act_link", "dve_link", "pool_link",
             "tanh_ready", "cols_ready", "mask_ready", "k0_ready", "k0_masked", "m0_ready", "m0_copied",
             "dt_ready", "au_ready", "trig_ready", "ab_ready", "arg_p", "arg_q", "prod_p", "prod_q",
             "exp_p", "exp_q", "sin_p", "sin_q", "p_done", "q1_done", "q2_done", "qc_done",
             "wvf_ready", "wvf_copied", "vw_ready", "vw_copied", "w1_scaled", "b1_ready", "b1_done",
             "kern_ready", "kern_copied", "skip_added", "freq_ready", "freq_copied",
             "low_built", "high_built", "t1_ready", "t1_copied", "wup_ready", "bup_ready", "wup_copied",
             "t2_ready", "t2_copied", "lowT_built", "highT_built", "wdn_ready", "wdn_copied",
             "k1_ready", "k1_masked", "ctxrep_ready", "v1_ready", "v1_masked", "misc_ready", "bup_done"]
        s = {x: sem(x) for x in n}

        def readers(name, b):
            if name.startswith("cen"):
                i = int(name[3:])
                return [(normed[i], b + 1)]
            if name.startswith("var"):
                i = int(name[3:])
                return [(rs_done, VARS.index((name, b)) + 1)]
            if name.startswith("score"):
                g = NT * b + int(name[5:])
                return [(s["topk_step"], 32 * g + 8), (s["exps_done"], g + 1)]
            if name.startswith("sA"):
                g = NT * b + int(name[2])
                return [(s["shifted"], 3 * g + int(name[4]) + 1)]
            if name.startswith("tA"):
                g = NT * b + int(name[2])
                return [(s["probsT_copied"], 3 * g + int(name[4]) + 1)]
            if name.startswith("oA"):
                return [(s["pv_scaled"], NT * b + int(name[2]) + 1)]
            if name.startswith("up"):
                return [(s["up_gelu"], HT * b + int(name[2]) + 1)]
            if name.startswith("fup"):
                return [(s["fup_gelu"], HT * b + int(name[3]) + 1)]
            if name.startswith("kern"):
                return [(s["kern_copied"], int(name[4:]) + 1)]
            if name.startswith("m0_"):
                return [(s["m0_copied"], int(name[3:]) + 1)]
            if name.startswith("t1_"):
                return [(s["t1_copied"], 2)]
            return {
                "attnT": [(s["attnT_copied"], b + 1)], "fa": [(s["filmed"], b + 1)], "fb": [(s["filmed"], b + 1)],
                "xt": [(s["xt_copied"], b + 1)], "d0": [(s["dft_copied"], 2 * b + 1)],
                "d1": [(s["dft_copied"], 2 * b + 2)], "y": [(x_ready["xt2"], b + 1)],
                "fc": [(s["ao_ready"], b + 1)], "fd": [(x_ready["xt2"], b + 1)],
                "down": [(x_ready["xt3"], b + 1)], "fdown": [(x_ready["x2"], b + 1)], "q": [(s["q_copied"], b + 1)],
                "outT": [(s["outT_copied"], b + 1)], "wo": [(x_ready["x3"], b + 1)],
                "logits": [(s["logits_copied"], b + 1)], "wT": [(s["wT_copied"], b + 1)],
                "ex0": [(s["experts_ready"], 2 * b + 1)], "ex1": [(s["experts_ready"], 2 * b + 2)],
                "u0": [(s["silu_ready"], 2 * b + 1)], "u1": [(s["silu_ready"], 2 * b + 2)],
                "v0": [(s["experts_ready"], 2 * b + 1)], "v1": [(s["experts_ready"], 2 * b + 2)],
                "moe": [(s["x4_ready"], b + 1)], "k0": [(s["k0_masked"], B)],
                "wvf": [(s["wvf_copied"], 1)], "vw": [(s["vw_copied"], b + 1)],
                "w1c": [(s["b1_done"], 1)], "fr0": [(s["freq_copied"], 1)], "fr1": [(s["freq_copied"], 2)],
                "wup": [(s["wup_copied"], 1)], "bup": [(s["bup_done"], 1)], "t2": [(s["t2_copied"], 1)],
                "wdn": [(s["wdn_copied"], 1)], "k1": [(s["k1_masked"], b + 1)],
                "v1a": [(s["v1_masked"], B - 1)], "v1b": [(s["v1_masked"], B)],
            }[name]

        block = ctx.enter_context(nc.Block())

        @block.sync
        def _(sp):
            sp.dma_start(packs["first"][0][:, :], dram["first"]).then_inc(loaded["first"], 16)
            sp.dma_start(X[:, 0, :], dram["x"][0]).then_inc(x_loaded[0], 16)
            sp.dma_start(packs["small"][0][:, :], dram["small"]).then_inc(loaded["small"], 16)
            sp.dma_start(dskip[:, :], dram["dskip"]).then_inc(masks_loaded, 16)
            sp.dma_start(vmask8[:, :], dram["vmask"]).then_inc(masks_loaded, 16)
            sp.dma_start(tmask8[:, :], dram["tmask"]).then_inc(masks_loaded, 16)
            for name in ("kgen", "film"):
                sp.dma_start(packs[name][0][:, :], dram[name]).then_inc(loaded[name], 16)
            sp.dma_start(X[:, 1, :], dram["x"][1]).then_inc(x_loaded[1], 16)
            for name in ("dft", "ffn", "bfly"):
                sp.dma_start(packs[name][0][:, :], dram[name]).then_inc(loaded[name], 16)
            for b in range(2, B):
                sp.dma_start(X[:, b, :], dram["x"][b]).then_inc(x_loaded[b], 16)
            for name in ("att1", "moe"):
                sp.dma_start(packs[name][0][:, :], dram[name]).then_inc(loaded[name], 16)
            for b in range(B):
                sp.wait_ge(s["x4_ready"], b + 1)
                sp.dma_start(out_dram[b], X[:, b, :]).then_inc(stored, 16)
            sp.wait_ge(stored, 16 * B)

        @block.tensor
        def _(pe):
            C, J, I = part("first", "C"), part("first", "J"), part("first", "I")

            def claim(name, b):
                former = BEFORE[name, b]
                if former is not None:
                    for semaphore, value in readers(*former):
                        pe.wait_ge(semaphore, value)
                return bank(name, b)

            def mm(out, lhsT, rhs, start=True, stop=True, **kw):
                return nc.tensor.matmul(out, lhsT, rhs, start=start, stop=stop, **kw)

            def center(i, b):
                src = {0: X, 1: LO, 2: LO, 3: X, 4: X, 5: X}[i]
                ready = [(x_loaded[b], 16), (x_ready["xt2"], b + 1), (x_ready["xt3"], b + 1),
                         (x_ready["x1"], b + 1), (x_ready["x2"], b + 1), (x_ready["x3"], b + 1)][i]
                if i == 0 and b == 0:
                    pe.wait_ge(loaded["first"], 16)
                pe.wait_ge(*ready)
                src = XT2 if i in (1, 2) else X
                mm(claim(f"cen{i}", b)[:, :], C, src[:, b, :]).then_inc(centered, 1)

            def var(i, b):
                pe.wait_ge(squared, CENTERS.index((f"center{i}", b)) + 1)
                mm(claim(f"var{i}", b)[:, :], J, SQ[:, b, :]).then_inc(variance, 1)

            XT2 = XG
            for step, b in SCHEDULE:
                tile = int(step[-1]) if step[-1].isdigit() else 0
                g = NT * b + tile
                if step.startswith("center"):
                    center(tile, b)
                elif step.startswith("var"):
                    var(tile, b)
                elif step.startswith("scoreA"):
                    t = slice(P * tile, P * tile + P)
                    if tile == 0:
                        pe.wait_ge(s["q_copied"], b + 1)
                        pe.wait_ge(s["k1_masked"], b + 1)
                    for n, (h, k) in enumerate(GROUPS):
                        mm(claim(f"sA{tile}_{n}", b)[:, 0:k * SK], Q1[:, b, t], k1bd[:, b % 2, h:h + k, :])\
                            .then_inc(s["scoresA_ready"], 1)
                elif step.startswith("score"):
                    if tile == 0:
                        pe.wait_ge(normed[0], b + 1)
                        if b == 0:
                            pe.wait_ge(s["m0_copied"], B)
                            pe.wait_ge(s["mask_ready"], 1)
                    o = claim(f"score{tile}", b)[:, 0:H0 * SK]
                    mm(o, XN[:, b % 2, P * tile:P * tile + P], M0[:, b, :], stop=False)
                    mm(o, ones_bf[:, :], maskrow[:, b, :], start=False).then_inc(s["scores_ready"], 1)
                elif step == "attnT":
                    pe.wait_ge(s["attn_summed"], NT * (b + 1))
                    o = claim("attnT", b)
                    for t in range(NT):
                        last = nc.tensor.transpose(o[0:SK, P * t:P * t + P], ASUM[:, b % 2, t, :], I)
                    last.then_inc(s["attnT_ready"], 1)
                elif step == "vw":
                    if b == 0:
                        pe.wait_ge(s["wvf_copied"], 1)
                    mm(claim("vw", b)[0:SK, :], part("first", "ctx", DC)[:, SK * b:SK * b + SK], wvf[:, :])\
                        .then_inc(s["vw_ready"], 1)
                elif step == "film_in":
                    pe.wait_ge(s["attnT_copied"], b + 1)
                    pe.wait_ge(s["vw_copied"], b + 1)
                    for j, name in enumerate(("fa", "fb")):
                        mm(claim(name, b)[:, :], VW[:, b % 2, P * j:P * j + P], AT[:, b % 2, :]).then_inc(s["film_in_ready"], 1)
                elif step == "xt":
                    pe.wait_ge(s["filmed"], b + 1)
                    o = claim("xt", b)
                    for t in range(NT):
                        last = nc.tensor.transpose(o[:, P * t:P * t + P], XG[:, b, P * t:P * t + P], I)
                    last.then_inc(s["xt_ready"], 1)
                elif step == "dft":
                    if b == 0:
                        pe.wait_ge(loaded["dft"], 16)
                    pe.wait_ge(s["xt_copied"], b + 1)
                    x = XTM[:, b % 2, :, :].rearrange("p (c j) d -> p c j d", j=2)
                    for ft in range(2):
                        o = claim(f"d{ft}", b)
                        for cs in range(2):
                            w = part("dft", "near")[:, 512 * cs:512 * cs + 512].rearrange("p (a f) -> p a f", a=2)
                            for j in range(2):
                                last = mm(o[:, 256 * cs:256 * cs + 256], w[:, j, P * ft:P * ft + P], x[:, :, j, :],
                                          start=j == 0, stop=j == 1)
                        last.then_inc(s["dft_ready"], 1)
                elif step == "idft":
                    pe.wait_ge(s["mixed_y"], b + 1)
                    pe.wait_ge(s["mixed_z"], b + 1)
                    o = claim("y", b)
                    for c in range(2):
                        for n in range(4):
                            ri, ft = divmod(n, 2)
                            w = part("dft", ("icos", "isin")[ri])[:, CH * ft:CH * ft + CH]
                            last = mm(o[:, CH * c:CH * c + CH], YZ[:, ri, ft, c, :], w,
                                      start=n == 0, stop=n == 3)
                    last.then_inc(s["y_ready"], 1)
                elif step == "film_out":
                    for j, name in enumerate(("fc", "fd")):
                        mm(claim(name, b)[:, :], VW[:, b % 2, 256 + P * j:256 + P * j + P], AT[:, b % 2, :])\
                            .then_inc(s["film_out_ready"], 1)
                elif step == "ffn_up":
                    pe.wait_ge(normed[1], b + 1)
                    if b == 0:
                        pe.wait_ge(s["w1_scaled"], 1)
                    for j in range(HT):
                        mm(claim(f"up{j}", b)[:, :], w1g[:, P * j:P * j + P], LO[:, b, :]).then_inc(s["up_ready"], 1)
                elif step == "ffn_down":
                    o = claim("down", b)
                    for j in range(HT):
                        pe.wait_ge(s["up_gelu"], HT * b + j + 1)
                        last = mm(o[:, :], part("ffn", "w2")[:, P * j:P * j + P], HIDB[:, 0, j, :],
                                  start=j == 0, stop=j == HT - 1)
                    last.then_inc(s["down_ready"], 1)
                elif step == "fold_up":
                    pe.wait_ge(normed[3], b + 1)
                    if b == 0:
                        pe.wait_ge(s["wup_copied"], 1)
                    for j in range(HT):
                        mm(claim(f"fup{j}", b)[:, :], wupf[:, P * j:P * j + P], LO[:, b, :]).then_inc(s["fup_ready"], 1)
                elif step == "fold_down":
                    o = claim("fdown", b)
                    if b == 0:
                        pe.wait_ge(s["wdn_copied"], 1)
                    for j in range(HT):
                        pe.wait_ge(s["fup_gelu"], HT * b + j + 1)
                        last = mm(o[:, :], wdnf[:, j, :], HIDB[:, 1, j, :], start=j == 0, stop=j == HT - 1)
                    last.then_inc(s["fdown_ready"], 1)
                elif step == "q":
                    pe.wait_ge(normed[4], b + 1)
                    mm(claim("q", b)[:, :], part("att1", "wqT"), LO[:, b, :]).then_inc(s["q_ready"], 1)
                elif step.startswith("mixA"):
                    pe.wait_ge(s["probs_ready"], 3 * g + 3)
                    for n in range(3):
                        o = claim(f"tA{tile}_{n}", b)
                        for c in range(4 * n, min(4 * n + 4, NCH)):
                            k = CROWS[c]
                            last = nc.tensor.transpose(o[0:k, P * (c - 4 * n):P * (c - 4 * n) + P],
                                                       PR[:, g % 2, P * c:P * c + k], I)
                        last.then_inc(s["probsT_ready"], 1)
                    if g == 0:
                        pe.wait_ge(s["v1_masked"], B)
                    o = claim(f"oA{tile}", b)
                    for c in range(NCH):
                        if c % 4 == 0:
                            pe.wait_ge(s["probsT_copied"], 3 * g + c // 4 + 1)
                        k, h, m = CROWS[c], CH0[c], CHN[c]
                        last = mm(o[:, VW9 * h:VW9 * (h + m)], PT[0:k, g % 2, c, :], v9[0:k, b, c, 0:VW9 * m],
                                  start=c == 0, stop=c == NCH - 1, skip_group_check=True)
                    last.then_inc(s["pv_ready"], 1)
                elif step == "outT":
                    pe.wait_ge(s["pv_scaled"], NT * (b + 1))
                    o = claim("outT", b)
                    for t in range(NT):
                        last = nc.tensor.transpose(o[:, P * t:P * t + P], OT[:, b % 2, t, :], I)
                    last.then_inc(s["outT_ready"], 1)
                elif step == "wo":
                    pe.wait_ge(s["outT_copied"], b + 1)
                    if b == 0:
                        pe.wait_ge(s["misc_ready"], 1)
                    mm(claim("wo", b)[:, :], woT1[:, :], OTT[:, :]).then_inc(s["wo_ready"], 1)
                elif step == "logits":
                    pe.wait_ge(normed[5], b + 1)
                    o = claim("logits", b)
                    for t in range(NT):
                        last = mm(o[:, NE * t:NE * t + NE], LO[:, b, P * t:P * t + P], part("moe", "gate"))
                    last.then_inc(s["logits_ready"], 1)
                elif step == "expand":
                    pe.wait_ge(s["gate_ready"], b + 1)
                    o = claim("wT", b)
                    for t in range(NT):
                        last = nc.tensor.transpose(o[0:3 * NE, P * t:P * t + P], G3[:, b % 2, t, :], I)
                    last.then_inc(s["wT_ready"], 1)
                    pe.wait_ge(s["wT_copied"], b + 1)
                    for j in range(2):
                        mm(claim(f"ex{j}", b)[:, :], expand[:, P * j:P * j + P], WT[:, b % 2, :])\
                            .then_inc(s["expand_ready"], 1)
                elif step == "experts":
                    for j in range(2):
                        mm(claim(f"u{j}", b)[:, :], part("moe", "wu")[:, P * j:P * j + P], LO[:, b, :])\
                            .then_inc(s["u_ready"], 1)
                        mm(claim(f"v{j}", b)[:, :], part("moe", "wv")[:, P * j:P * j + P], LO[:, b, :])\
                            .then_inc(s["v_ready"], 1)
                elif step == "moe_out":
                    o = claim("moe", b)
                    for j in range(2):
                        pe.wait_ge(s["experts_ready"], 2 * b + j + 1)
                        last = mm(o[:, :], wom[:, j, :], SU[:, j, :], start=j == 0, stop=j == 1)
                    last.then_inc(s["moe_ready"], 1)
                elif step == "s_k0":
                    pe.wait_ge(loaded["first"], 16)
                    mm(claim("k0", 0)[:, 0:B * SK], part("first", "wk0", DC), part("first", "ctx", DC)).then_inc(s["k0_ready"], 1)
                elif step == "s_m0":
                    for i in range(B):
                        pe.wait_ge(s["k0_masked"], i + 1)
                        mm(claim(f"m0_{i}", 0)[:, 0:H0 * SK], part("first", "wqT0"), k0bd[:, i, :, :]).then_inc(s["m0_ready"], 1)
                elif step == "s_vw":
                    pe.wait_ge(loaded["film"], 16)
                    mm(claim("wvf", 0)[0:DC, :], part("film", "wvT"), part("film", "film")).then_inc(s["wvf_ready"], 1)
                elif step == "s_w1":
                    pe.wait_ge(loaded["ffn"], 16)
                    o = claim("w1c", 0)
                    for j in range(HT):
                        last = mm(o[:, j:j + 1], part("ffn", "w1")[:, P * j:P * j + P], part("small", "bffn"))
                    last.then_inc(s["b1_ready"], 1)
                elif step.startswith("s_kern"):
                    if tile == 0:
                        pe.wait_ge(s["p_done"], 1)
                        pe.wait_ge(s["qc_done"], 1)
                    o = claim(f"kern{tile}", 0)
                    for i in range(32):
                        d = 32 * tile + i
                        last = mm(o[0:L1, L2 * i:L2 * i + L2], big[0][:, L1 * d:L1 * d + L1],
                                  big[3][:, 2048 + L2 * d:2048 + L2 * d + L2])
                    last.then_inc(s["kern_ready"], 1)
                elif step == "s_freq":
                    pe.wait_ge(loaded["dft"], 16)
                    pe.wait_ge(s["kern_copied"], 4)
                    pe.wait_ge(s["skip_added"], 1)
                    for full in range(2):
                        o = claim(f"fr{full}", 0)
                        for cs in range(2):
                            w = [part("dft", x)[:, 512 * cs:512 * cs + 512].rearrange("p (a f) -> p a f", a=2)
                                 for x in ("near", "tail")]
                            for ft in range(2):
                                c0 = 256 * cs + P * ft
                                na = 4 if full else 2
                                for a in range(na):
                                    last = mm(o[:, c0:c0 + P], w[a // 2][:, a % 2, P * ft:P * ft + P], KT[:, a, :],
                                              start=a == 0, stop=a == na - 1)
                        last.then_inc(s["freq_ready"], 1)
                elif step == "s_bfly1":
                    pe.wait_ge(s["low_built"], 1)
                    w = part("bfly", "wexpT").rearrange("p (k m) -> p k m", k=4)
                    for n in range(2):
                        o = claim(f"t1_{n}", 0)
                        for j in range(2):
                            last = mm(o[:, 256 * j:256 * j + P + 1], bdl[:, 2 * n + j, :], w[:, 2 * n + j, :])
                        last.then_inc(s["t1_ready"], 1)
                elif step == "s_bfly2":
                    pe.wait_ge(s["high_built"], 1)
                    pe.wait_ge(s["t1_copied"], 2)
                    o = claim("wup", 0)
                    for j in range(4):
                        last = mm(o[:, :], t1s[:, j, 0:P], bdh[:, j, :], start=j == 0, stop=j == 3)
                    last.then_inc(s["wup_ready"], 1)
                    o = claim("bup", 0)
                    for m in range(4):
                        for j in range(4):
                            last = mm(o[:, m:m + 1], bdh[:, j, P * m:P * m + P], t1s[:, j, P:P + 1],
                                      start=j == 0, stop=j == 3)
                    last.then_inc(s["bup_ready"], 1)
                    pe.wait_ge(s["highT_built"], 1)
                    o = claim("t2", 0)
                    w = part("bfly", "wcon").rearrange("p (k m) -> p k m", k=4)
                    for m in range(4):
                        for j in range(4):
                            last = mm(o[:, P * m:P * m + P], bdh[:, j, P * m:P * m + P], w[:, j, :],
                                      start=j == 0, stop=j == 3)
                    last.then_inc(s["t2_ready"], 1)
                elif step == "s_bfly3":
                    pe.wait_ge(s["lowT_built"], 1)
                    pe.wait_ge(s["t2_copied"], 1)
                    o = claim("wdn", 0)
                    for m in range(4):
                        last = mm(o[:, P * m:P * m + P], bdl[:, m, :], t2s[:, m, :])
                    last.then_inc(s["wdn_ready"], 1)
                elif step == "k1":
                    if b == 0:
                        pe.wait_ge(loaded["att1"], 16)
                    mm(claim("k1", b)[:, 0:SK], part("att1", "wkT", DC + 1), part("first", "ctx", DC + 1)[:, SK * b:SK * b + SK])\
                        .then_inc(s["k1_ready"], 1)
                elif step == "s_v1":
                    for i in range(B):
                        pe.wait_ge(s["ctxrep_ready"], 1)
                        name = ("v1a", "v1b")[i % 2]
                        if i < 2:
                            o = claim(name, 0)
                        else:
                            pe.wait_ge(s["v1_masked"], i - 1)
                            o = bank(name, 0)
                        for c in range(NCH):
                            at = P * c % SK
                            last = mm(o[0:CROWS[c], 27 * c:27 * c + VW9 * CHN[c]], ctxrep[:, i, at:at + CROWS[c]],
                                      part("att1", "wv9", DC + 1)[:, VW9 * CH0[c]:VW9 * (CH0[c] + CHN[c])])
                        last.then_inc(s["v1_ready"], 1)

        @block.scalar
        def _(act):
            XT2 = XG
            link = [0]

            table_of = {ACT.Exp: 6, ACT.Ln: 6, ACT.Gelu: 10, ACT.Silu: 18, ACT.Sin: 18, ACT.Tanh: 18}
            table = [None]

            def a(out, in_, func, **kw):
                need = table_of.get(func, table[0])
                if need != table[0]:
                    nc.scalar.add_instruction(mybir.InstLoadActFuncSet(
                        name=nc.get_next_instruction_name(), act_func_set_id=need, ins=[], outs=[]))
                    table[0] = need
                return nc.scalar.activation(out, in_, func, **kw)

            def linked(ins):
                link[0] += 1
                return ins.then_inc(s["act_link"], 1)

            def settle(back=0):
                act.wait_ge(s["act_link"], link[0] - back)

            for step, b in SCHEDULE:
                tile = int(step[-1]) if step[-1].isdigit() else 0
                g = NT * b + tile
                if step.startswith("center"):
                    act.wait_ge(centered, CENTERS.index((step, b)) + 1)
                    a(SQ[:, b, :], bank(f"cen{tile}", b)[:, :], ACT.Square).then_inc(squared, 1)
                elif step.startswith("var"):
                    act.wait_ge(variance, VARS.index((step, b)) + 1)
                    v = bank(f"var{tile}", b)[:, :]
                    at = VARS.index((step, b))
                    if at >= 2:
                        former, e = VARS[at - 2]
                        act.wait_ge(normed[int(former[-1])], e + 1)
                    if b == 0 and tile == 0:
                        act.wait_ge(s["cols_ready"], 1)
                    linked(a(RS[:, VARS.index((step, b)) % 2, :], v, ACT.Ln, bias=cst[:, 0:1]))
                    if tile == 0:
                        if b >= 1:
                            act.wait_ge(normed[0], b)
                        linked(a(R12[:, :], v, ACT.Ln, bias=cst[:, 1:2]))
                        settle(1)
                        linked(a(RS[:, VARS.index((step, b)) % 2, :], RS[:, VARS.index((step, b)) % 2, :], ACT.Exp, scale=-0.5))
                        settle(1)
                        a(R12[:, :], R12[:, :], ACT.Exp, scale=-0.5).then_inc(rs_done, 1)
                    else:
                        settle()
                        a(RS[:, VARS.index((step, b)) % 2, :], RS[:, VARS.index((step, b)) % 2, :], ACT.Exp, scale=-0.5).then_inc(rs_done, 1)
                elif step.startswith("scoreA"):
                    for n, (h, k) in enumerate(GROUPS):
                        act.wait_ge(s["shifted"], 3 * g + n + 1)
                        x = PR[:, g % 2, SK * h:SK * (h + k)]
                        a(x, x, ACT.Exp).then_inc(s["probs_ready"], 1)
                elif step.startswith("score"):
                    act.wait_ge(s["negmax_ready"], g + 1)
                    if g >= 2:
                        act.wait_ge(s["selected"], g - 1)
                    for h in range(H0):
                        last = a(E0[:, g % 2, h, :], bank(step, b)[:, SK * h:SK * h + SK], ACT.Exp,
                                 bias=negm[:, g % 2, h:h + 1])
                    last.then_inc(s["exps_done"], 1)
                elif step == "attnT":
                    act.wait_ge(s["attnT_ready"], b + 1)
                    if b >= 2:
                        act.wait_ge(s["film_out_ready"], 2 * (b - 1))
                    a(AT[:, b % 2, :], bank("attnT", b)[0:SK, :], ACT.Copy).then_inc(s["attnT_copied"], 1)
                elif step == "vw":
                    act.wait_ge(s["vw_ready"], b + 1)
                    if b >= 2:
                        act.wait_ge(s["film_out_ready"], 2 * (b - 1))
                    a(VW[:, b % 2, :], bank("vw", b)[0:SK, :], ACT.Copy).then_inc(s["vw_copied"], 1)
                elif step == "xt":
                    act.wait_ge(s["xt_ready"], b + 1)
                    if b >= 2:
                        act.wait_ge(s["dft_ready"], 2 * (b - 1))
                    a(XTM[:, b % 2, :, :].rearrange("p t d -> p (t d)"), bank("xt", b)[:, :], ACT.Copy).then_inc(s["xt_copied"], 1)
                elif step == "dft":
                    if b >= 1:
                        act.wait_ge(s["mixed_y"], b)
                        act.wait_ge(s["mixed_z"], b)
                    for ft in range(2):
                        act.wait_ge(s["dft_ready"], 2 * b + ft + 1)
                        a(XF[:, ft, :, :, :].rearrange("p s c d -> p (s c d)"), bank(f"d{ft}", b)[:, :], ACT.Copy)\
                            .then_inc(s["dft_copied"], 1)
                elif step == "film_out":
                    act.wait_ge(s["film_out_ready"], 2 * b + 1)
                    if b >= 1:
                        act.wait_ge(x_ready["xt2"], b)
                    a(AO[:, :], bank("fc", b)[:, :], ACT.Identity, bias=filmb[:, 2:3]).then_inc(s["ao_ready"], 1)
                elif step == "ffn_up":
                    if b == 0:
                        act.wait_ge(s["b1_done"], 1)
                    if b >= 1:
                        act.wait_ge(s["down_ready"], b)
                    for j in range(HT):
                        act.wait_ge(s["up_ready"], HT * b + j + 1)
                        a(HIDB[:, 0, j, :], bank(f"up{j}", b)[:, :], ACT.Gelu, bias=b1f[:, j:j + 1]).then_inc(s["up_gelu"], 1)
                elif step == "fold_up":
                    if b == 0:
                        act.wait_ge(s["bup_done"], 1)
                    if b >= 1:
                        act.wait_ge(s["fdown_ready"], b)
                    for j in range(HT):
                        act.wait_ge(s["fup_ready"], HT * b + j + 1)
                        a(HIDB[:, 1, j, :], bank(f"fup{j}", b)[:, :], ACT.Gelu, bias=bup[:, j:j + 1]).then_inc(s["fup_gelu"], 1)
                elif step == "q":
                    act.wait_ge(s["q_ready"], b + 1)
                    a(Q1[:, b, :], bank("q", b)[:, :], ACT.Identity, bias=part("small", "bq")).then_inc(s["q_copied"], 1)
                elif step.startswith("mixA"):
                    if g >= 2:
                        act.wait_ge(s["pv_ready"], g - 1)
                    for n in range(3):
                        act.wait_ge(s["probsT_ready"], 3 * g + n + 1)
                        o = bank(f"tA{tile}_{n}", b)
                        dst = PT[:, g % 2, :, :].rearrange("p c t -> p (c t)")
                        if n < 2:
                            a(dst[:, 512 * n:512 * n + 512], o[:, :], ACT.Copy).then_inc(s["probsT_copied"], 1)
                        else:
                            a(dst[:, 1024:1152], o[:, 0:P], ACT.Copy)
                            a(dst[0:CROWS[9], 1152:1280], o[0:CROWS[9], P:2 * P], ACT.Copy).then_inc(s["probsT_copied"], 1)
                elif step == "outT":
                    act.wait_ge(s["outT_ready"], b + 1)
                    if b >= 1:
                        act.wait_ge(s["wo_ready"], b)
                    a(OTT[:, :], bank("outT", b)[:, :], ACT.Copy).then_inc(s["outT_copied"], 1)
                elif step == "logits":
                    act.wait_ge(s["logits_ready"], b + 1)
                    if b == 0:
                        act.wait_ge(s["misc_ready"], 1)
                    if b >= 2:
                        act.wait_ge(s["gate_ready"], b - 1)
                    a(LG[:, b % 2, :, 0:NE], bank("logits", b)[:, 0:NT * NE].rearrange("p (t e) -> p t e", t=NT), ACT.Copy)\
                        .then_inc(s["logits_copied"], 1)
                elif step == "top2":
                    act.wait_ge(s["shift_ready"], b + 1)
                    a(GE[:, b % 2, :, :], GE[:, b % 2, :, :], ACT.Exp).then_inc(s["gate_exp"], 1)
                elif step == "expand":
                    act.wait_ge(s["wT_ready"], b + 1)
                    if b >= 2:
                        act.wait_ge(s["expand_ready"], 2 * (b - 1))
                    a(WT[:, b % 2, :], bank("wT", b)[0:3 * NE, :], ACT.Copy).then_inc(s["wT_copied"], 1)
                elif step == "experts":
                    if b >= 1:
                        act.wait_ge(s["moe_ready"], b)
                    for j in range(2):
                        act.wait_ge(s["u_ready"], 2 * b + j + 1)
                        a(SU[:, j, :], bank(f"u{j}", b)[:, :], ACT.Silu).then_inc(s["silu_ready"], 1)
                elif step == "s_cols":
                    act.wait_ge(loaded["small"], 16)
                    a(tanhs[:, :], packs["small"][0][:, SMALL["gx0"][0]:SMALL["gf1"][1]], ACT.Tanh).then_inc(s["tanh_ready"], 1)
                elif step == "s_m0":
                    for i in range(B):
                        act.wait_ge(s["m0_ready"], i + 1)
                        a(M0[:, i, :], bank(f"m0_{i}", 0)[:, 0:H0 * SK], ACT.Copy).then_inc(s["m0_copied"], 1)
                elif step == "s_kgen0":
                    act.wait_ge(loaded["kgen"], 16)
                    a(kt["dt"], part("kgen", "logdt"), ACT.Exp).then_inc(s["dt_ready"], 1)
                    act.wait_ge(s["au_ready"], 1)
                    a(kt["th"], kt["a"], ACT.Tanh, scale=0.5)
                    a(kt["sb"], kt["v"], ACT.Sin, scale=6.283185)
                    a(kt["q"], kt["v"], ACT.Sin, scale=3.1415925).then_inc(s["trig_ready"], 1)
                elif step == "s_kgen1":
                    act.wait_ge(s["prod_q"], 1)
                    a(big[3][:, 2048:4096], big[3][:, 2048:4096], ACT.Exp).then_inc(s["exp_q"], 1)
                    act.wait_ge(s["prod_p"], 1)
                    a(big[1][:, :], big[1][:, :], ACT.Exp).then_inc(s["exp_p"], 1)
                    act.wait_ge(s["arg_q"], 1)
                    a(big[2][:, 0:2048], big[2][:, 0:2048], ACT.Sin, scale=6.283185, bias=cst[:, 2:3])
                    a(big[2][:, 2048:4096], big[2][:, 2048:4096], ACT.Sin, scale=6.283185).then_inc(s["sin_q"], 1)
                elif step == "s_kgen2":
                    act.wait_ge(s["arg_p"], 1)
                    a(big[0][:, :], big[0][:, :], ACT.Sin, scale=6.283185, bias=part("small", "sin_bias")).then_inc(s["sin_p"], 1)
                elif step == "s_vw":
                    act.wait_ge(s["wvf_ready"], 1)
                    a(wvf[:, :], bank("wvf", 0)[0:DC, :], ACT.Copy, scale=part("small", "mod_gate", DC)).then_inc(s["wvf_copied"], 1)
                elif step.startswith("s_kern"):
                    act.wait_ge(s["kern_ready"], tile + 1)
                    o = bank(f"kern{tile}", 0)[0:L1, :].rearrange("p (d a q) -> p q a d", a=4, q=4)
                    for q in range(4):
                        last = a(KT[32 * q:32 * q + 32, :, 32 * tile:32 * tile + 32], o[:, q, :, :], ACT.Copy)
                    last.then_inc(s["kern_copied"], 1)
                elif step == "s_freq":
                    act.wait_ge(s["freq_ready"], 1)
                    a(H0f[:, :, :, :].rearrange("p s f d -> p (s f d)"), bank("fr0", 0)[:, :], ACT.Copy).then_inc(s["freq_copied"], 1)
                    act.wait_ge(s["freq_ready"], 2)
                    a(H1f[:, :, :, :].rearrange("p s f d -> p (s f d)"), bank("fr1", 0)[:, :], ACT.Copy,
                      scale=part("small", "sgnf")).then_inc(s["freq_copied"], 1)
                elif step == "s_bfly1":
                    for n in range(2):
                        act.wait_ge(s["t1_ready"], n + 1)
                        a(t1s[:, 2 * n:2 * n + 2, :],
                          bank(f"t1_{n}", 0)[:, :].rearrange("p (j m) -> p j m", j=2)[:, :, 0:P + 1], ACT.Copy)\
                            .then_inc(s["t1_copied"], 1)
                elif step == "s_bfly2":
                    act.wait_ge(s["wup_ready"], 1)
                    a(wupf[:, :], bank("wup", 0)[:, :], ACT.Copy).then_inc(s["wup_copied"], 1)
                    act.wait_ge(s["t2_ready"], 1)
                    a(t2s[:, :, :].rearrange("p m d -> p (m d)"), bank("t2", 0)[:, :], ACT.Copy).then_inc(s["t2_copied"], 1)
                elif step == "s_bfly3":
                    act.wait_ge(s["wdn_ready"], 1)
                    act.wait_ge(s["tanh_ready"], 1)
                    a(wdnf[:, :, :].rearrange("p m d -> p (m d)"), bank("wdn", 0)[:, :], ACT.Copy, scale=tanhs[:, 1:2])\
                        .then_inc(s["wdn_copied"], 1)

        @block.vector
        def _(dve):
            XT2 = XG
            link = [0]

            def tt(out, x, y, op):
                return nc.vector.tensor_tensor(out, x, y, op)

            def ts(out, x, s1, s2, op0, op1=None):
                if op1 is None:
                    return nc.vector.tensor_scalar(out, x, s1, None, op0)
                return nc.vector.tensor_scalar(out, x, s1, s2, op0, op1)

            def stt(out, x, sc, y, op0, op1, **kw):
                return nc.vector.scalar_tensor_tensor(out, x, sc, y, op0, op1, **kw)

            def chain(ins):
                link[0] += 1
                ins.then_inc(s["dve_link"], 1)
                dve.wait_ge(s["dve_link"], link[0])

            def linked(ins):
                link[0] += 1
                return ins.then_inc(s["dve_link"], 1)

            def settle(back=0):
                dve.wait_ge(s["dve_link"], link[0] - back)

            for step, b in SCHEDULE:
                tile = int(step[-1]) if step[-1].isdigit() else 0
                g = NT * b + tile
                if step.startswith("var"):
                    dve.wait_ge(rs_done, VARS.index((step, b)) + 1)
                    cen = bank(f"cen{tile}", b)[:, :]
                    if tile == 0:
                        if b >= 2:
                            dve.wait_ge(x_ready["xt2"], b - 1)
                        linked(tt(XG[:, b, :], cen, R12[:, :], ALU.mult))
                        tt(XN[:, b % 2, :], cen, RS[:, VARS.index((step, b)) % 2, :], ALU.mult).then_inc(normed[0], 1)
                    else:
                        tt(LO[:, b, :], cen, RS[:, VARS.index((step, b)) % 2, :], ALU.mult).then_inc(normed[tile], 1)
                elif step.startswith("scoreA"):
                    if g >= 2:
                        dve.wait_ge(s["probsT_ready"], 3 * (g - 1))
                    for n, (h, k) in enumerate(GROUPS):
                        dve.wait_ge(s["scoresA_ready"], 3 * g + n + 1)
                        o = bank(f"sA{tile}_{n}", b)[:, 0:k * SK].rearrange("p (h k) -> p h k", h=k)
                        m = mx1[:, g % 2, h:h + k]
                        chain(nc.vector.tensor_reduce(m, o, AX.X, ALU.max))
                        tt(PR[:, g % 2, SK * h:SK * (h + k)].rearrange("p (h k) -> p h k", h=k), o,
                           m.unsqueeze(2).broadcast_to([P, k, SK]), ALU.subtract).then_inc(s["shifted"], 1)
                elif step.startswith("score"):
                    dve.wait_ge(s["scores_ready"], g + 1)
                    sc = bank(step, b)
                    base = 32 * g
                    for r in range(4):
                        for h in range(H0):
                            src = sc[:, SK * h:SK * h + SK] if r == 0 else R8[:, g % 2, (r - 1) % 2, h, :]
                            n = 8 * r + h
                            if n >= 4:
                                dve.wait_ge(s["topk_step"], base + n - 3)
                            nc.vector.max(V8[:, g % 2, h, r, :], src).then_inc(s["topk_step"], 1)
                        for h in range(H0):
                            src = sc[:, SK * h:SK * h + SK] if r == 0 else R8[:, g % 2, (r - 1) % 2, h, :]
                            n = 8 * r + 4 + h
                            dve.wait_ge(s["topk_step"], base + n - 3)
                            nc.vector.match_replace(R8[:, g % 2, r % 2, h, :], V8[:, g % 2, h, r, :], src, NEG)\
                                .then_inc(s["topk_step"], 1)
                        if r == 0:
                            if g >= 2:
                                dve.wait_ge(s["exps_done"], g - 1)
                            ts(negm[:, g % 2, :], V8[:, g % 2, :, 0, 0], -1.0, None, ALU.mult).then_inc(s["negmax_ready"], 1)
                elif step.startswith("weigh"):
                    dve.wait_ge(s["exps_done"], g + 1)
                    dve.wait_ge(s["topk_step"], 32 * (g + 1))
                    if g >= 2:
                        dve.wait_ge(s["attn_summed"], g - 1)
                    stt(sel[:, g % 2, :, :], R8[:, g % 2, 1, :, :], -1.0e38, E0[:, g % 2, :, :], ALU.is_le, ALU.mult)\
                        .then_inc(s["selected"], 1)
                    dve.wait_ge(s["selected"], g + 1)
                    chain(nc.vector.tensor_reduce(sm[:, 0, :], sel[:, g % 2, :, :], AX.X, ALU.add))
                    chain(nc.vector.reciprocal(sm[:, 1, :], sm[:, 0, :]))
                    ts(w4[:, g % 2, :], sm[:, 1, :], tm4[:, g:g + 1], None, ALU.mult).then_inc(s["weights_ready"], 1)
                elif step == "film_in":
                    dve.wait_ge(s["film_in_ready"], 2 * b + 1)
                    dve.wait_ge(s["affined"], b + 1)
                    chain(stt(XG[:, b, :], bank("fa", b)[:, :], filmb[:, 0:1], XG[:, b, :], ALU.add, ALU.mult))
                    dve.wait_ge(s["film_in_ready"], 2 * b + 2)
                    stt(XG[:, b, :], bank("fb", b)[:, :], filmb[:, 1:2], XG[:, b, :], ALU.add, ALU.add).then_inc(s["filmed"], 1)
                elif step == "mix":
                    dve.wait_ge(s["dft_copied"], 2 * b + 2)
                    if b == 0:
                        dve.wait_ge(s["freq_copied"], 2)
                    if b >= 1:
                        dve.wait_ge(s["y_ready"], b)
                    xf = XF
                    both = lambda t: t.unsqueeze(2).broadcast_to([P, 2, 2, D])
                    y = YZ[:, 0, :, :, :]
                    m0 = MT[:, 0, :, :].rearrange("p f (c d) -> p f c d", c=2)
                    m1 = MT[:, 1, :, :].rearrange("p f (c d) -> p f c d", c=2)
                    linked(tt(m0, xf[:, :, 0, :, :], both(H0f[:, 0, :, :]), ALU.mult))
                    chain(tt(m1, xf[:, :, 1, :, :], both(H0f[:, 1, :, :]), ALU.mult))
                    chain(tt(y, m0, m1, ALU.subtract))
                    linked(tt(m0[:, :, 0, :], xf[:, :, 0, 0, :], H1f[:, 1, :, :], ALU.mult))
                    linked(tt(m1[:, :, 0, :], xf[:, :, 1, 0, :], H1f[:, 0, :, :], ALU.mult))
                    settle(1)
                    chain(tt(y[:, :, 1, :], y[:, :, 1, :], m0[:, :, 0, :], ALU.add))
                    tt(y[:, :, 1, :], y[:, :, 1, :], m1[:, :, 0, :], ALU.add).then_inc(s["mixed_y"], 1)
                elif step == "film_out":
                    dve.wait_ge(s["y_ready"], b + 1)
                    dve.wait_ge(s["ao_ready"], b + 1)
                    chain(tt(XT2[:, b, :], bank("y", b)[:, :], AO[:, :], ALU.mult))
                    dve.wait_ge(s["film_out_ready"], 2 * b + 2)
                    chain(stt(XT2[:, b, :], bank("fd", b)[:, :], filmb[:, 3:4], XT2[:, b, :], ALU.add, ALU.add))
                    tt(XT2[:, b, :], XT2[:, b, :], XN[:, b % 2, :], ALU.add).then_inc(x_ready["xt2"], 1)
                elif step == "ffn_down":
                    dve.wait_ge(s["down_ready"], b + 1)
                    stt(XT2[:, b, :], bank("down", b)[:, :], part("small", "b2"), XT2[:, b, :], ALU.add, ALU.add)\
                        .then_inc(x_ready["xt3"], 1)
                elif step == "x1":
                    dve.wait_ge(s["scaled_out"], b + 1)
                    tt(X[:, b, :], X[:, b, :], LO[:, b, :], ALU.add).then_inc(x_ready["x1"], 1)
                elif step == "fold_down":
                    dve.wait_ge(s["fdown_ready"], b + 1)
                    stt(X[:, b, :], bank("fdown", b)[:, :], bdn[:, 0:1], X[:, b, :], ALU.add, ALU.add).then_inc(x_ready["x2"], 1)
                elif step.startswith("mixA"):
                    dve.wait_ge(s["pv_ready"], g + 1)
                    if b >= 2 and tile == 0:
                        dve.wait_ge(s["outT_ready"], b - 1)
                    o = bank(f"oA{tile}", b)[:, 0:H1 * VW9].rearrange("p (h e) -> p h e", e=VW9)
                    chain(nc.vector.reciprocal(rec1[:, g % 2, :], o[:, :, DH1]))
                    tt(OT[:, b % 2, tile, :].rearrange("p (h e) -> p h e", e=DH1), o[:, :, 0:DH1],
                       rec1[:, g % 2, :].unsqueeze(2).broadcast_to([P, H1, DH1]), ALU.mult).then_inc(s["pv_scaled"], 1)
                elif step == "wo":
                    dve.wait_ge(s["wo_ready"], b + 1)
                    if b == 0:
                        dve.wait_ge(s["misc_ready"], 1)
                    stt(X[:, b, :], bank("wo", b)[:, :], bo1[:, 0:1], X[:, b, :], ALU.add, ALU.add).then_inc(x_ready["x3"], 1)
                elif step == "top2":
                    p2 = b % 2
                    dve.wait_ge(s["logits_copied"], b + 1)
                    for t in range(NT):
                        linked(nc.vector.max(G8[:, p2, t, :], LG[:, p2, t, 0:NE]))
                    settle()
                    linked(nc.vector.tensor_copy(GR[:, p2, :, 0:2], G8[:, p2, :, 0:2]))
                    if b >= 2:
                        dve.wait_ge(s["gate_exp"], b - 1)
                    tt(GE[:, p2, :, :], LG[:, p2, :, 0:NE], G8[:, p2, :, 0:1].broadcast_to([P, NT, NE]), ALU.subtract)\
                        .then_inc(s["shift_ready"], 1)
                    settle()
                    for t in range(NT):
                        linked(nc.vector.match_replace(LR[:, p2, t, :], GR[:, p2, t, :], LG[:, p2, t, :], NEG))
                    settle()
                    dve.wait_ge(s["gate_exp"], b + 1)
                    chain(stt(GS[:, p2, :, :], LR[:, p2, :, 0:NE], -2.5e38, GE[:, p2, :, :], ALU.is_le, ALU.mult))
                    chain(nc.vector.tensor_reduce(gsum[:, p2, :], GS[:, p2, :, :], AX.X, ALU.add))
                    chain(nc.vector.reciprocal(gsum[:, p2, :], gsum[:, p2, :]))
                    chain(tt(GW[:, p2, :, :], GS[:, p2, :, :], gsum[:, p2, :].unsqueeze(2).broadcast_to([P, NT, NE]), ALU.mult))
                    hi, mid = GB[:, p2, 0, :, :], GB[:, p2, 1, :, :]
                    if b >= 2:
                        dve.wait_ge(s["wT_ready"], b - 1)
                    chain(nc.vector.tensor_copy(hi, GW[:, p2, :, :]))
                    linked(nc.vector.tensor_copy(G3[:, p2, :, 0:NE], hi))
                    chain(tt(GS[:, p2, :, :], GW[:, p2, :, :], hi, ALU.subtract))
                    chain(nc.vector.tensor_copy(mid, GS[:, p2, :, :]))
                    linked(nc.vector.tensor_copy(G3[:, p2, :, NE:2 * NE], mid))
                    tt(G3[:, p2, :, 2 * NE:3 * NE], GS[:, p2, :, :], mid, ALU.subtract).then_inc(s["gate_ready"], 1)
                elif step == "experts":
                    for j in range(2):
                        dve.wait_ge(s["silu_ready"], 2 * b + j + 1)
                        dve.wait_ge(s["v_ready"], 2 * b + j + 1)
                        x = SU[:, j, :]
                        chain(tt(x, bank(f"v{j}", b)[:, :], x, ALU.mult))
                        dve.wait_ge(s["expand_ready"], 2 * b + j + 1)
                        tt(x, bank(f"ex{j}", b)[:, :], x, ALU.mult).then_inc(s["experts_ready"], 1)
                elif step == "moe_out":
                    dve.wait_ge(s["moe_ready"], b + 1)
                    tt(X[:, b, :], bank("moe", b)[:, :], X[:, b, :], ALU.add).then_inc(s["x4_ready"], 1)
                elif step == "s_cols":
                    linked(nc.vector.memset(cst[:, 0:1], EPS))
                    linked(nc.vector.memset(cst[:, 1:2], EPS * EPS / (1.0 + EPS)))
                    linked(nc.vector.memset(cst[:, 2:3], 0.25 * 6.283185))
                    linked(nc.vector.memset(maskrow[:, :, :], 0.0))
                    linked(nc.vector.memset(ones_bf[:, :], 1.0))
                    dve.wait_ge(masks_loaded, 48)
                    settle()
                    linked(nc.vector.tensor_copy(maskf[:, :, :], vmask8[:, :].rearrange("p (b k) -> p b k", b=B)))
                    linked(nc.vector.tensor_copy(tm4[:, :], tmask8[:, :]))
                    settle()
                    linked(ts(maskf[:, :, :], maskf[:, :, :], -1.0, -MASKED, ALU.add, ALU.mult))
                    linked(ts(tm4[:, :], tm4[:, :], 1.0 / H0, None, ALU.mult))
                    settle()
                    for i in range(B):
                        last = nc.vector.tensor_copy(maskrow[0:1, i, :].rearrange("p (h k) -> p h k", h=H0),
                                                     maskf[:, i, :].unsqueeze(1).broadcast_to([1, H0, SK]))
                    last.then_inc(s["mask_ready"], 1)
                    dve.wait_ge(s["tanh_ready"], 1)
                    linked(ts(gin2[:, :], part("small", "gin"), float((1.0 + EPS) ** -0.5), None, ALU.mult))
                    linked(stt(filmb[:, :], part("small", "bfilm"), part("small", "mod_gate"), part("small", "film_one"),
                               ALU.mult, ALU.add))
                    linked(tt(gA[:, :], part("small", "gno"), tanhs[:, 0:1], ALU.mult))
                    linked(tt(bA[:, :], part("small", "bno"), tanhs[:, 0:1], ALU.mult))
                    chain(tt(bdn[:, :], part("small", "bcon"), part("small", "dbias"), ALU.add))
                    tt(bdn[:, :], bdn[:, :], tanhs[:, 1:2], ALU.mult).then_inc(s["cols_ready"], 1)
                elif step == "s_k0":
                    dve.wait_ge(s["k0_ready"], 1)
                    for i in range(B):
                        tt(k0bd[:, i, :, :],
                           bank("k0", 0)[:, SK * i:SK * i + SK].unsqueeze(1).broadcast_to([P, H0, SK]),
                           part("small", "hmask0").unsqueeze(2).broadcast_to([P, H0, SK]), ALU.mult).then_inc(s["k0_masked"], 1)
                elif step == "s_kgen0":
                    k = kt
                    ar, ai = part("kgen", "are"), part("kgen", "aim")
                    dve.wait_ge(s["dt_ready"], 1)
                    linked(tt(k["a"], k["dt"], ar, ALU.mult))
                    chain(stt(k["u"], k["dt"], float(1.0 / (2.0 * np.pi)), ai, ALU.mult, ALU.mult))
                    chain(ts(k["k"], k["u"], MAGIC, MAGIC, ALU.add, ALU.subtract))
                    tt(k["v"], k["u"], k["k"], ALU.subtract).then_inc(s["au_ready"], 1)
                    linked(tt(k["m"], ar, ar, ALU.mult))
                    chain(tt(k["t1"], ai, ai, ALU.mult))
                    chain(tt(k["m"], k["m"], k["t1"], ALU.add))
                    chain(nc.vector.reciprocal(k["t3"], k["m"]))
                    dve.wait_ge(s["trig_ready"], 1)
                    chain(ts(k["t1"], k["th"], -1.0, 1.0, ALU.mult, ALU.add))
                    chain(nc.vector.reciprocal(k["t2"], k["t1"]))
                    chain(stt(k["em"], k["th"], 2.0, k["t2"], ALU.mult, ALU.mult))
                    chain(tt(k["t1"], k["q"], k["q"], ALU.mult))
                    linked(ts(k["t2"], k["t1"], -2.0, 1.0, ALU.mult, ALU.add))
                    linked(stt(k["ei"], k["em"], 1.0, k["sb"], ALU.add, ALU.mult))
                    settle(1)
                    chain(tt(k["t4"], k["em"], k["t2"], ALU.mult))
                    chain(stt(k["er"], k["t1"], -2.0, k["t4"], ALU.mult, ALU.add))
                    linked(tt(k["t1"], k["er"], ar, ALU.mult))
                    linked(tt(k["t2"], k["ei"], ai, ALU.mult))
                    linked(tt(k["al"], k["ei"], ar, ALU.mult))
                    linked(tt(k["be"], k["er"], ai, ALU.mult))
                    settle(2)
                    linked(tt(k["t1"], k["t1"], k["t2"], ALU.add))
                    settle(1)
                    linked(tt(k["al"], k["al"], k["be"], ALU.subtract))
                    settle(1)
                    linked(tt(k["gr"], k["t1"], k["t3"], ALU.mult))
                    settle(1)
                    linked(tt(k["gi"], k["al"], k["t3"], ALU.mult))
                    c1, c2, sg = part("kgen", "c1"), part("kgen", "c2"), part("small", "sgn2")
                    settle()
                    linked(stt(k["t1"], c1, sg, k["gr"], ALU.mult, ALU.mult))
                    linked(stt(k["t2"], c2, -2.0, k["gi"], ALU.mult, ALU.mult))
                    linked(stt(k["t4"], c1, sg, k["gi"], ALU.mult, ALU.mult))
                    linked(stt(k["em"], c2, -2.0, k["gr"], ALU.mult, ALU.mult))
                    settle(2)
                    linked(tt(k["al"], k["t1"], k["t2"], ALU.add))
                    settle(1)
                    tt(k["be"], k["em"], k["t4"], ALU.subtract).then_inc(s["ab_ready"], 1)
                elif step == "s_kgen1":
                    v = kt["v"].unsqueeze(2).broadcast_to([P, D, L2])
                    l2 = part("kgen", "l2row").unsqueeze(1).broadcast_to([P, D, L2])
                    ph, ph2 = big[2][:, 0:2048], big[2][:, 2048:4096]
                    rnd, r2 = big[0][:, 0:2048], big[0][:, 2048:4096]
                    dve.wait_ge(s["au_ready"], 1)
                    chain(tt(ph.rearrange("p (d l) -> p d l", d=D), v, l2, ALU.mult))
                    linked(ts(rnd, ph, 0.25, MAGIC, ALU.add, ALU.add))
                    chain(ts(r2, ph, MAGIC, None, ALU.add))
                    chain(stt(ph2, r2, MAGIC, ph, ALU.subtract, ALU.subtract, reverse1=True))
                    stt(ph, rnd, MAGIC, ph, ALU.subtract, ALU.subtract, reverse1=True).then_inc(s["arg_q"], 1)
                elif step == "s_kgen2":
                    v = kt["v"].unsqueeze(2).broadcast_to([P, D, L1])
                    l1 = part("kgen", "l1row").unsqueeze(1).broadcast_to([P, D, L1])
                    be = kt["be"].unsqueeze(2).broadcast_to([P, D, L2])
                    as3 = lambda t: t.rearrange("p (d l) -> p d l", d=D)
                    dve.wait_ge(s["sin_q"], 1)
                    dve.wait_ge(s["ab_ready"], 1)
                    chain(tt(as3(big[2][:, 2048:4096]), as3(big[2][:, 2048:4096]), be, ALU.mult))
                    dve.wait_ge(s["q1_done"], 1)
                    tt(big[3][:, 0:2048], big[2][:, 2048:4096], big[2][:, 0:2048], ALU.add).then_inc(s["q2_done"], 1)
                    chain(tt(as3(big[0][:, :]), v, l1, ALU.mult))
                    dve.wait_ge(s["q2_done"], 1)
                    chain(ts(big[2][:, :], big[0][:, :], part("small", "sin_off"), MAGIC, ALU.add, ALU.add))
                    stt(big[0][:, :], big[2][:, :], MAGIC, big[0][:, :], ALU.subtract, ALU.subtract, reverse1=True)\
                        .then_inc(s["arg_p"], 1)
                    dve.wait_ge(s["sin_p"], 1)
                    dve.wait_ge(s["exp_p"], 1)
                    tt(big[0][:, :], big[0][:, :], big[1][:, :], ALU.mult).then_inc(s["p_done"], 1)
                elif step == "s_w1":
                    dve.wait_ge(s["b1_ready"], 1)
                    ts(w1g, w1g, part("small", "gffn"), None, ALU.mult).then_inc(s["w1_scaled"], 1)
                    tt(b1f[:, :], bank("w1c", 0)[:, 0:HT], part("small", "b1"), ALU.add).then_inc(s["b1_done"], 1)
                elif step == "s_kern3":
                    dve.wait_ge(s["kern_copied"], 4)
                    tt(KT[0:1, 0, :], KT[0:1, 0, :], dskip[:, :], ALU.add).then_inc(s["skip_added"], 1)
                elif step == "s_bfly2":
                    dve.wait_ge(s["bup_ready"], 1)
                    tt(bup[:, :], bank("bup", 0)[:, 0:4], part("small", "upb"), ALU.add).then_inc(s["bup_done"], 1)
                elif step == "k1":
                    dve.wait_ge(s["k1_ready"], b + 1)
                    if b >= 2:
                        dve.wait_ge(s["scoresA_ready"], 3 * NT * (b - 1))
                    tt(k1bd[:, b % 2, :, :], bank("k1", b)[:, 0:SK].unsqueeze(1).broadcast_to([P, H1, SK]),
                       part("small", "hmask1").unsqueeze(2).broadcast_to([P, H1, SK]), ALU.mult).then_inc(s["k1_masked"], 1)
                elif step == "s_v1":
                    vm = part("att1", "vmask")
                    for i in range(B):
                        dve.wait_ge(s["v1_ready"], i + 1)
                        o = bank(("v1a", "v1b")[i % 2], 0)
                        vv = v9[:, i, :, :].rearrange("p c e -> p (c e)")
                        tt(vv[:, 0:243], o[:, 0:243], vm[:, 0:243], ALU.mult)
                        tt(vv[0:CROWS[9], 243:261], o[0:CROWS[9], 243:261], vm[0:CROWS[9], 243:261], ALU.mult)\
                            .then_inc(s["v1_masked"], 1)
                elif step == "s_misc":
                    linked(nc.vector.memset(LG[:, :, :, NE:14], NEG))
                    linked(nc.vector.memset(GR[:, :, :, 2:8], NEG))
                    dve.wait_ge(loaded["moe"], 16)
                    linked(ts(part("moe", "wo"), part("moe", "wo"), tanhs[:, 3:4], None, ALU.mult))
                    dve.wait_ge(loaded["att1"], 16)
                    linked(nc.vector.tensor_copy(expand[:, :], part("moe", "expand", 3 * NE)))
                    linked(ts(woT1, woT1, tanhs[:, 2:3], None, ALU.mult))
                    tt(bo1[:, :], part("small", "bo"), tanhs[:, 2:3], ALU.mult).then_inc(s["misc_ready"], 1)

        @block.gpsimd
        def _(pool):
            link = [0]

            def chain(ins):
                link[0] += 1
                ins.then_inc(s["pool_link"], 1)
                pool.wait_ge(s["pool_link"], link[0])

            def tt(out, x, y, op):
                return nc.gpsimd.tensor_tensor(out, x, y, op)

            def butterfly(which, half, transposed):
                width, count, state = (32, LOW, bflyl) if half == "low" else (16, HIGH, bflyh)
                w = part("bfly", which + half)
                ident = part("bfly", "idl" if half == "low" else "idh")
                n = 4 * width
                for i in range(count):
                    st = count - 1 - i if transposed else i
                    src = ident if i == 0 else state[:, (i - 1) % 2, :, :].rearrange("p a b -> p (a b)")
                    dst = state[:, i % 2, :, :].rearrange("p a b -> p (a b)")
                    q = 2 ** st
                    y = src.rearrange("p (n o q) -> p n o q", o=2, q=q)
                    ws = w[:, 2 * n * st:2 * n * (st + 1)].rearrange("p (n q o i) -> p n o i q", q=q, o=2, i=2)
                    m = n // (2 * q)
                    for x, t in ((0, bt1), (1, bt2)):
                        wx = ws[:, :, x, :, :] if transposed else ws[:, :, :, x, :]
                        ins = tt(t[:, 0:n].rearrange("p (n o q) -> p n o q", o=2, q=q),
                                 wx, y[:, :, x:x + 1, :].broadcast_to([P, m, 2, q]), ALU.mult)
                        if x == 1:
                            chain(ins)
                    chain(tt(dst, bt1[:, 0:n], bt2[:, 0:n], ALU.add))
                return state[:, (count - 1) % 2, :, :]

            def dense_low(which, transposed):
                y = butterfly(which, "low", transposed)
                for j in range(4):
                    last = tt(bdl[:, j, :].rearrange("p (k i) -> p k i", k=4),
                              y[:, j, :].unsqueeze(1).broadcast_to([P, 4, 32]),
                              part("bfly", "eye4").unsqueeze(2).broadcast_to([P, 4, 32]), ALU.mult)
                return last

            def dense_high(which, transposed):
                y = butterfly(which, "high", transposed)
                for j in range(4):
                    last = tt(bdh[:, j, :].rearrange("p (h l) -> p h l", h=16),
                              y[:, j, :].unsqueeze(2).broadcast_to([P, 16, 32]),
                              part("bfly", "eye32").unsqueeze(1).broadcast_to([P, 16, 32]), ALU.mult)
                return last

            for step, b in SCHEDULE:
                tile = int(step[-1]) if step[-1].isdigit() else 0
                g = NT * b + tile
                if step == "var0":
                    if b == 0:
                        pool.wait_ge(s["cols_ready"], 1)
                    pool.wait_ge(normed[0], b + 1)
                    nc.gpsimd.tensor_scalar(XG[:, b, :], XG[:, b, :], gin2[:, 0:1], part("small", "bin"),
                                            ALU.mult, ALU.add).then_inc(s["affined"], 1)
                elif step.startswith("weigh"):
                    pool.wait_ge(s["weights_ready"], g + 1)
                    chain(tt(dw[:, :, :], sel[:, g % 2, :, :], w4[:, g % 2, :].unsqueeze(2).broadcast_to([P, H0, SK]), ALU.mult))
                    chain(tt(a2[:, :, :], dw[:, 0:2, :], dw[:, 2:4, :], ALU.add))
                    if b >= 2 and tile == 0:
                        pool.wait_ge(s["attnT_ready"], b - 1)
                    tt(ASUM[:, b % 2, tile, :], a2[:, 0, :], a2[:, 1, :], ALU.add).then_inc(s["attn_summed"], 1)
                    pool.wait_ge(s["attn_summed"], g + 1)
                elif step == "mix":
                    pool.wait_ge(s["dft_copied"], 2 * b + 2)
                    if b == 0:
                        pool.wait_ge(s["freq_copied"], 2)
                    if b >= 1:
                        pool.wait_ge(s["y_ready"], b)
                    xf = XF
                    both = lambda t: t.unsqueeze(2).broadcast_to([P, 2, 2, D])
                    z = YZ[:, 1, :, :, :]
                    m0 = MT[:, 2, :, :].rearrange("p f (c d) -> p f c d", c=2)
                    m1 = MT[:, 3, :, :].rearrange("p f (c d) -> p f c d", c=2)
                    tt(m0, xf[:, :, 1, :, :], both(H0f[:, 0, :, :]), ALU.mult)
                    chain(tt(m1, xf[:, :, 0, :, :], both(H0f[:, 1, :, :]), ALU.mult))
                    chain(tt(z, m0, m1, ALU.add))
                    tt(m0[:, :, 0, :], xf[:, :, 1, 0, :], H1f[:, 1, :, :], ALU.mult)
                    chain(tt(m1[:, :, 0, :], xf[:, :, 0, 0, :], H1f[:, 0, :, :], ALU.mult))
                    chain(tt(z[:, :, 1, :], z[:, :, 1, :], m0[:, :, 0, :], ALU.add))
                    tt(z[:, :, 1, :], z[:, :, 1, :], m1[:, :, 0, :], ALU.subtract).then_inc(s["mixed_z"], 1)
                    pool.wait_ge(s["mixed_z"], b + 1)
                elif step == "x1":
                    pool.wait_ge(normed[2], b + 1)
                    nc.gpsimd.tensor_scalar(LO[:, b, :], LO[:, b, :], gA[:, 0:1], bA[:, 0:1], ALU.mult, ALU.add)\
                        .then_inc(s["scaled_out"], 1)
                elif step == "s_kgen1":
                    a3 = lambda n: kt["a"].unsqueeze(2).broadcast_to([P, D, n])
                    as3 = lambda t: t.rearrange("p (d l) -> p d l", d=D)
                    pool.wait_ge(s["au_ready"], 1)
                    tt(as3(big[3][:, 2048:4096]), a3(L2), part("kgen", "l2row").unsqueeze(1).broadcast_to([P, D, L2]), ALU.mult)\
                        .then_inc(s["prod_q"], 1)
                    tt(as3(big[1][:, :]), a3(L1), part("kgen", "l1row").unsqueeze(1).broadcast_to([P, D, L1]), ALU.mult)\
                        .then_inc(s["prod_p"], 1)
                elif step == "s_kgen2":
                    as3 = lambda t: t.rearrange("p (d l) -> p d l", d=D)
                    al = kt["al"].unsqueeze(2).broadcast_to([P, D, L2])
                    pool.wait_ge(s["sin_q"], 1)
                    pool.wait_ge(s["ab_ready"], 1)
                    pool.wait_ge(s["exp_q"], 1)
                    tt(as3(big[2][:, 0:2048]), as3(big[2][:, 0:2048]), al, ALU.mult).then_inc(s["q1_done"], 1)
                    pool.wait_ge(s["q2_done"], 1)
                    tt(big[3][:, 2048:4096], big[3][:, 0:2048], big[3][:, 2048:4096], ALU.mult).then_inc(s["qc_done"], 1)
                elif step == "s_bfly0":
                    pool.wait_ge(loaded["bfly"], 16)
                    pool.wait_ge(s["kern_ready"], 4)
                    dense_low("u", False).then_inc(s["low_built"], 1)
                    pool.wait_ge(s["low_built"], 1)
                    dense_high("u", False).then_inc(s["high_built"], 1)
                    pool.wait_ge(s["high_built"], 1)
                elif step == "s_bfly2":
                    pool.wait_ge(s["t1_ready"], 2)
                    pool.wait_ge(s["bup_ready"], 1)
                    dense_high("d", True).then_inc(s["highT_built"], 1)
                    pool.wait_ge(s["highT_built"], 1)
                    dense_low("d", True).then_inc(s["lowT_built"], 1)
                    pool.wait_ge(s["lowT_built"], 1)
                elif step == "s_v1":
                    pool.wait_ge(s["k1_ready"], 1)
                    nc.gpsimd.tensor_copy(ctxrep.rearrange("p b (r k) -> p b r k", r=3),
                                          part("first", "ctx", DC + 1).rearrange("p (b k) -> p b k", b=B).unsqueeze(2)
                                          .broadcast_to([DC + 1, B, 3, SK])).then_inc(s["ctxrep_ready"], 1)



def kernel(**inputs):
    import concourse.bacc as _bacc
    from concourse.bass_utils import run_bass_kernel_spmd as _run

    a = {k: np.asarray(v) for k, v in inputs.items()}
    f = np.float32

    def rows(x, n=P):
        x = np.asarray(x, f)
        out = np.zeros((n,) + x.shape[1:], f)
        out[:x.shape[0]] = x
        return out

    def col(x):
        return np.asarray(x, f).reshape(-1, 1)

    def tiles(x):
        x = np.asarray(x, f)
        return np.ascontiguousarray(x.reshape(-1, P, x.shape[1]).transpose(1, 0, 2)).reshape(P, -1)

    def every(x):
        return np.full((P, 1), 1.0, f) if x is None else np.broadcast_to(np.asarray(x, f).reshape(1, 1), (P, 1))

    def pack(cols, n, parts):
        out = np.zeros((P, n), f)
        for name, v in parts.items():
            lo, hi = cols[name]
            assert v.shape == (P, hi - lo), (name, v.shape, hi - lo)
            out[:, lo:hi] = v
        assert set(parts) == set(cols), set(cols) ^ set(parts)
        return out

    p = np.arange(P)
    ident = np.eye(P, dtype=f)
    upper = (p < NS)
    gx, gf = a["g_xattn"], a["g_ffn"]
    small = pack(SMALL, N_SMALL, {
        "mod_gate": every(a["L0_xattn_mod_gate"]), "gx0": every(gx[0]), "gf0": every(gf[0]),
        "gx1": every(gx[1]), "gf1": every(gf[1]),
        "gin": col(a["L0_xattn_g_norm_in"]), "bin": col(a["L0_xattn_b_norm_in"]),
        "bfilm": np.concatenate([a["L0_xattn_b_film_in"].reshape(2, D).T, a["L0_xattn_b_film_out"].reshape(2, D).T], 1),
        "film_one": np.tile(np.array([[1, 0, 1, 0]], f), (P, 1)),
        "gffn": col(a["L0_xattn_g_ffn"]), "bffn": col(a["L0_xattn_b_ffn"]),
        "b1": a["L0_xattn_b1"].reshape(HT, P).T, "b2": col(a["L0_xattn_b2"]),
        "gno": col(a["L0_xattn_g_norm_out"]), "bno": col(a["L0_xattn_b_norm_out"]),
        "upb": a["L0_ffn_up_bias"].reshape(HT, P).T, "bcon": col(a["L0_ffn_b_con"]), "dbias": col(a["L0_ffn_down_bias"]),
        "bq": col(a["L1_xattn_bq"]), "bo": col(a["L1_xattn_bo"]),
        "sin_off": col(np.where(upper, 0.25, 0.0)), "sgn2": col(np.where(upper, 2.0, -2.0)),
        "sgnf": col(np.where(p % 2 == 0, 1.0, -1.0)), "sin_bias": col(np.where(upper, 0.25 * 6.283185, 0.0)),
        "hmask0": (p[:, None] // DH0 == np.arange(H0)[None, :]).astype(f) * f(1.0 / np.sqrt(DH0)),
        "hmask1": (p[:, None] // DH1 == np.arange(H1)[None, :]).astype(f) * f(1.0 / np.sqrt(DH1)),
    })
    ctxT = np.zeros((P, B, SK), f)
    ctxT[:DC] = a["ctx_768"].transpose(2, 0, 1)
    ctxT[DC] = 1.0
    first = pack(FIRST, N_FIRST, {
        "C": ident - f(1.0 / D), "J": np.full((P, P), 1.0 / D, f), "I": ident,
        "wqT0": np.asarray(a["L0_xattn_Wq"]).T, "wk0": rows(a["L0_xattn_Wk"]), "ctx": ctxT.reshape(P, -1),
    })
    twice = lambda x: np.concatenate([np.asarray(x, f).T, np.asarray(x, f).T], 0)
    kgen = pack(KGEN, N_KGEN, {
        "logdt": np.broadcast_to(a["L0_xattn_log_dt"][None, :], (P, D)),
        "are": twice(a["L0_xattn_A_re"]), "aim": twice(a["L0_xattn_A_im"]),
        "c1": np.concatenate([a["L0_xattn_C_re"].T, a["L0_xattn_C_im"].T], 0),
        "c2": np.concatenate([a["L0_xattn_C_im"].T, a["L0_xattn_C_re"].T], 0),
        "l1row": np.broadcast_to(np.arange(L1, dtype=f), (P, L1)),
        "l2row": np.broadcast_to(L1 * np.arange(L2, dtype=f), (P, L2)),
    })
    film = pack(FILM, N_FILM, {
        "wvT": np.asarray(a["L0_xattn_Wv"]).T,
        "film": np.concatenate([a["L0_xattn_W_film_in"], a["L0_xattn_W_film_out"]], 1),
    })
    lag, freq = np.arange(S, dtype=np.float64), np.arange(CH, dtype=np.float64) + 0.5
    turn = 2.0 * np.pi * np.outer(lag, freq) / (2 * CH)
    inv = 2.0 * np.pi * np.outer(freq, lag[:CH]) / (2 * CH)
    dft = pack(DFT, N_DFT, {
        "near": np.concatenate([tiles(np.cos(turn[:CH])), tiles(np.sin(turn[:CH]))], 1),
        "tail": np.concatenate([tiles(np.cos(turn[CH:])), tiles(np.sin(turn[CH:]))], 1),
        "icos": tiles(np.cos(inv) / CH), "isin": tiles(np.sin(inv) / CH)})
    ffn = pack(FFN, N_FFN, {"w1": np.asarray(a["L0_xattn_W1"]), "w2": tiles(a["L0_xattn_W2"])})

    def low(w):
        w = np.asarray(w)[:LOW].reshape(LOW, 4, 4, 16, 4)
        w = w.transpose(2, 0, 1, 3, 4).reshape(4, 1, -1)
        return np.broadcast_to(w, (4, 32, w.shape[2])).reshape(P, -1)

    def high(w):
        w = np.asarray(w)[LOW:].reshape(HIGH, 1, 8, 32, 4)
        w = np.broadcast_to(w, (HIGH, 4, 8, 32, 4)).transpose(3, 0, 1, 2, 4).reshape(1, 32, -1)
        return np.broadcast_to(w, (4, 32, w.shape[2])).reshape(P, -1)

    idl = (p[:, None] % 32 == np.arange(32)[None, :]).astype(f)
    idh = (4 * np.arange(4)[None, :, None] + (p // 32)[:, None, None] == np.arange(16)[None, None, :]).astype(f)
    wexp = np.concatenate([a["L0_ffn_W_exp"].T, col(a["L0_ffn_b_exp"])], 1)
    bfly = pack(BFLY, N_BFLY, {
        "idl": np.tile(idl, (1, 4)), "idh": idh.reshape(P, -1), "eye32": idl,
        "eye4": ((p // 32)[:, None] == np.arange(4)[None, :]).astype(f),
        "ulow": low(a["L0_ffn_up_weights"]), "dlow": low(a["L0_ffn_down_weights"]),
        "uhigh": high(a["L0_ffn_up_weights"]), "dhigh": high(a["L0_ffn_down_weights"]),
        "wexpT": tiles(wexp), "wcon": tiles(a["L0_ffn_W_con"]),
    })
    wk = rows(np.concatenate([a["L1_xattn_Wk"].T, a["L1_xattn_bk"][None, :]], 0))
    wv9 = np.zeros((P, H1, VW9), f)
    wv9[:DC, :, :DH1] = a["L1_xattn_Wv"].T.reshape(DC, H1, DH1)
    wv9[DC, :, :DH1] = a["L1_xattn_bv"].reshape(H1, DH1)
    wv9[DC, :, DH1] = 1.0
    flat = P * np.arange(NCH)[None, :] + p[:, None]
    vmask = (flat[:, :, None] // SK == np.array(CH0)[None, :, None] + np.arange(3)[None, None, :]).astype(f)
    att1 = pack(ATT1, N_ATT1, {
        "wkT": wk, "wqT": np.asarray(a["L1_xattn_Wq"]).T, "woT": np.asarray(a["L1_xattn_Wo"]).T,
        "wv9": wv9.reshape(P, -1), "vmask": np.repeat(vmask[..., None], VW9, 3).reshape(P, -1),
    })
    expand = rows((np.arange(3 * NE)[:, None] % NE == (np.arange(NE * RE) // RE)[None, :]).astype(f))
    moe = pack(MOE, N_MOE, {
        "gate": np.asarray(a["L1_ffn_gate_w"]),
        "wu": a["L1_ffn_Wu"].transpose(1, 0, 2).reshape(D, -1), "wv": a["L1_ffn_Wv"].transpose(1, 0, 2).reshape(D, -1),
        "wo": tiles(a["L1_ffn_Wo"].reshape(NE * RE, D)), "expand": expand,
    })
    arrays = {
        "x": np.ascontiguousarray(a["x"].transpose(0, 2, 1)), "small": small, "first": first, "kgen": kgen,
        "film": film, "dft": dft, "ffn": ffn, "bfly": bfly, "att1": att1, "moe": moe,
        "vmask": np.ascontiguousarray(a["mask_BxS2_bf1"].reshape(1, -1)).view(np.uint8),
        "tmask": np.ascontiguousarray(a["mask_BxS_bf1"].reshape(B * NT, P).T).view(np.uint8),
        "dskip": np.ascontiguousarray(a["L0_xattn_D_skip"].reshape(1, D)),
    }
    nc = _bacc.Bacc("TRN2", target_bir_lowering=False, num_devices=1)
    dram = {n: nc.dram_tensor(f"in_{n}", v.shape, mybir.dt.from_np(v.dtype), kind="ExternalInput").ap()
            for n, v in arrays.items()}
    out = nc.dram_tensor("out_x", (B, D, S), mybir.dt.float32, kind="ExternalOutput").ap()
    build(nc, dram, out)
    r = _run(nc, [{f"in_{n}": v for n, v in arrays.items()}], core_ids=[0])
    return np.ascontiguousarray(np.asarray(r.results[0]["out_x"]).transpose(0, 2, 1))
```
